# Optimizing a Trainium2 kernel written in Bass

```python
import numpy as np
import jax
import jax.numpy as jnp

def _softmax(x, axis=-1):
    return jax.nn.softmax(x, axis=axis)
def _gelu(x):
    return jax.nn.gelu(x, approximate=True)
def _silu(x):
    return jax.nn.silu(x)
def _sigmoid(x):
    return jax.nn.sigmoid(x)
def _layernorm(x, axis=-1, eps=1e-5):
    m = jnp.mean(x, axis=axis, keepdims=True)
    v = jnp.var(x, axis=axis, keepdims=True)
    return (x - m) / jnp.sqrt(v + eps)
def _scatter_add(tgt, idx, src, axis=0):
    return tgt.at[idx].add(src)
def _segment_sum(src, seg, n):
    return jax.ops.segment_sum(src, seg, n)

kernel_name = 'mk_dlrm_tower_d1_rec_b0c5f4'

def setup_inputs(seed: int = 0):
    np.random.seed(seed)
    _w = jnp.asarray
    def _rec_inputs():
        import jax
        import jax.numpy as jnp
        _tk = jax.random.key(seed)
        dense_ctx = jax.random.normal(jax.random.fold_in(_tk, 190), (1024, 16), jnp.float32)
        ids = jnp.stack([jax.random.randint(jax.random.fold_in(_tk, 200 + f), (1024,), 0, v, jnp.int32) for f, v in enumerate([1000, 1000, 10000, 1000, 10000])], axis=1)
        tbl_0 = 0.05 * jax.random.normal(jax.random.fold_in(_tk, 500 + 0), (1000, 1024), jnp.float32)
        tbl_1 = 0.05 * jax.random.normal(jax.random.fold_in(_tk, 500 + 1), (1000, 1024), jnp.float32)
        tbl_2 = 0.05 * jax.random.normal(jax.random.fold_in(_tk, 500 + 2), (10000, 1024), jnp.float32)
        tbl_3 = 0.05 * jax.random.normal(jax.random.fold_in(_tk, 500 + 3), (1000, 1024), jnp.float32)
        tbl_4 = 0.05 * jax.random.normal(jax.random.fold_in(_tk, 500 + 4), (10000, 1024), jnp.float32)
        _rk = jax.random.fold_in(_tk, 7)
        W_top1 = 0.0155946 * jax.random.normal(jax.random.fold_in(_tk, 801), (4112, 512), jnp.float32)
        W_top2 = 0.0441942 * jax.random.normal(jax.random.fold_in(_tk, 802), (512, 256), jnp.float32)
        W_top3 = 0.0625 * jax.random.normal(jax.random.fold_in(_tk, 803), (256, 1), jnp.float32)
        b_top1 = jnp.zeros((512,), jnp.float32)
        b_top2 = jnp.zeros((256,), jnp.float32)
        return dense_ctx, ids, tbl_0, tbl_1, tbl_2, tbl_3, tbl_4, W_top1, b_top1, W_top2, b_top2, W_top3
    dense_ctx, ids, tbl_0, tbl_1, tbl_2, tbl_3, tbl_4, W_top1, b_top1, W_top2, b_top2, W_top3 = _rec_inputs()
    def _L0_rec_setup():
        import jax, jax.numpy as jnp
        import numpy as np
        B, D, H, T, NTE, NSE = (4096, 1024, 1024, 4, 2, 2)
        E = T * NTE + NSE
        K = NTE + NSE
        EXPERT_IN_IDX = np.minimum(np.arange(E) // NTE, T)
        SEL = np.array([[t * NTE + j for j in range(NTE)] + list(range(E - NSE, E)) for t in range(T)])

        def _ple_layer(x, W, b, Gw, Gb, Gsw=None, Gsb=None):
            xe = x[:, EXPERT_IN_IDX, :]
            eo = jax.nn.relu(jnp.einsum('bed,edh->beh', xe, W) + b)
            gates = jax.nn.softmax(jnp.einsum('btd,tdk->btk', x[:, :T, :], Gw) + Gb, axis=-1)
            sel_eo = eo[:, SEL, :]
            task_out = jnp.einsum('btk,btkh->bth', gates, sel_eo)
            if Gsw is None:
                return task_out
            gs = jax.nn.softmax(x[:, T, :] @ Gsw + Gsb, axis=-1)
            shared_out = jnp.einsum('be,beh->bh', gs, eo)
            return jnp.concatenate([task_out, shared_out[:, None, :]], axis=1)
        key = jax.random.key(seed)
        ks = jax.random.split(key, 8)
        s = 0.02
        return {'inputs': jax.random.normal(ks[0], (B, T + 1, D), jnp.float32), 'W0': jax.random.normal(ks[1], (E, D, H), jnp.float32) * s, 'b0': jnp.zeros((E, H), jnp.float32), 'G0w': jax.random.normal(ks[2], (T, D, K), jnp.float32) * s, 'G0b': jnp.zeros((T, K), jnp.float32), 'Gs0w': jax.random.normal(ks[3], (D, E), jnp.float32) * s, 'Gs0b': jnp.zeros((E,), jnp.float32), 'W1': jax.random.normal(ks[4], (E, H, H), jnp.float32) * s, 'b1': jnp.zeros((E, H), jnp.float32), 'G1w': jax.random.normal(ks[5], (T, H, K), jnp.float32) * s, 'G1b': jnp.zeros((T, K), jnp.float32)}
    _L0_rec_all = _L0_rec_setup()
    _L0_rec_in = {k: v for k, v in _L0_rec_all.items() if k in ('W0', 'b0', 'G0w', 'G0b', 'Gs0w', 'Gs0b', 'W1', 'b1', 'G1w', 'G1b', )}
    del _L0_rec_all

    return {
        "dense_ctx": dense_ctx,
        "ids": ids,
        "tbl_0": tbl_0,
        "tbl_1": tbl_1,
        "tbl_2": tbl_2,
        "tbl_3": tbl_3,
        "tbl_4": tbl_4,
        "W_top1": W_top1,
        "b_top1": b_top1,
        "W_top2": W_top2,
        "b_top2": b_top2,
        "W_top3": W_top3,
        "L0_rec_W0": _L0_rec_in["W0"],
        "L0_rec_b0": _L0_rec_in["b0"],
        "L0_rec_G0w": _L0_rec_in["G0w"],
        "L0_rec_G0b": _L0_rec_in["G0b"],
        "L0_rec_Gs0w": _L0_rec_in["Gs0w"],
        "L0_rec_Gs0b": _L0_rec_in["Gs0b"],
        "L0_rec_W1": _L0_rec_in["W1"],
        "L0_rec_b1": _L0_rec_in["b1"],
        "L0_rec_G1w": _L0_rec_in["G1w"],
        "L0_rec_G1b": _L0_rec_in["G1b"],
    }

def reference(dense_ctx, ids, tbl_0, tbl_1, tbl_2, tbl_3, tbl_4, W_top1, b_top1, W_top2, b_top2, W_top3, L0_rec_W0, L0_rec_b0, L0_rec_G0w, L0_rec_G0b, L0_rec_Gs0w, L0_rec_Gs0b, L0_rec_W1, L0_rec_b1, L0_rec_G1w, L0_rec_G1b):
    import jax
    import jax.numpy as jnp
    def _L0_rec_ref(inputs, W0, b0, G0w, G0b, Gs0w, Gs0b, W1, b1, G1w, G1b):
        import jax, jax.numpy as jnp
        import numpy as np
        B, D, H, T, NTE, NSE = (4096, 1024, 1024, 4, 2, 2)
        E = T * NTE + NSE
        K = NTE + NSE
        EXPERT_IN_IDX = np.minimum(np.arange(E) // NTE, T)
        SEL = np.array([[t * NTE + j for j in range(NTE)] + list(range(E - NSE, E)) for t in range(T)])

        def _ple_layer(x, W, b, Gw, Gb, Gsw=None, Gsb=None):
            xe = x[:, EXPERT_IN_IDX, :]
            eo = jax.nn.relu(jnp.einsum('bed,edh->beh', xe, W) + b)
            gates = jax.nn.softmax(jnp.einsum('btd,tdk->btk', x[:, :T, :], Gw) + Gb, axis=-1)
            sel_eo = eo[:, SEL, :]
            task_out = jnp.einsum('btk,btkh->bth', gates, sel_eo)
            if Gsw is None:
                return task_out
            gs = jax.nn.softmax(x[:, T, :] @ Gsw + Gsb, axis=-1)
            shared_out = jnp.einsum('be,beh->bh', gs, eo)
            return jnp.concatenate([task_out, shared_out[:, None, :]], axis=1)
        h = _ple_layer(inputs, W0, b0, G0w, G0b, Gs0w, Gs0b)
        return _ple_layer(h, W1, b1, G1w, G1b)

    e = jnp.stack([tbl_0[ids[:, 0]], tbl_1[ids[:, 1]], tbl_2[ids[:, 2]], tbl_3[ids[:, 3]], tbl_4[ids[:, 4]]], axis=1)
    z = _L0_rec_ref(e, L0_rec_W0, L0_rec_b0, L0_rec_G0w, L0_rec_G0b, L0_rec_Gs0w, L0_rec_Gs0b, L0_rec_W1, L0_rec_b1, L0_rec_G1w, L0_rec_G1b)
    z = z.reshape(z.shape[0], -1)
    h = jnp.concatenate([z, dense_ctx], axis=1)
    h = jnp.maximum(h @ W_top1 + b_top1, 0.0)
    h = jnp.maximum(h @ W_top2 + b_top2, 0.0)
    y = h @ W_top3
    return y


_drawn_inputs = setup_inputs


def setup_inputs(seed=0):
    import zlib

    import numpy as np

    out = dict(_drawn_inputs(seed))
    spreads = {'b_top1': (0.0, 0.1),
     'b_top2': (0.0, 0.1),
     'L0_rec_b0': (0.0, 0.1),
     'L0_rec_G0b': (0.0, 0.8),
     'L0_rec_Gs0b': (0.0, 0.8),
     'L0_rec_b1': (0.0, 0.1),
     'L0_rec_G1b': (0.0, 0.8)}
    factors = {'tbl_0': 8.0,
     'tbl_1': 8.0,
     'tbl_2': 8.0,
     'tbl_3': 8.0,
     'tbl_4': 8.0,
     'L0_rec_W0': 5.295,
     'L0_rec_G0w': 8.0,
     'L0_rec_Gs0w': 8.0,
     'L0_rec_G1w': 8.0}
    for name, (base, spread) in spreads.items():
        noise = np.random.default_rng([zlib.crc32(name.encode()), seed]).standard_normal(out[name].shape)
        drawn = base * np.exp(spread * noise) if base else spread * noise
        out[name] = jnp.asarray(drawn.astype(out[name].dtype))
    for name, factor in factors.items():
        out[name] = (out[name] * factor).astype(out[name].dtype)
    return out
```

```python
from contextlib import ExitStack

import numpy as np
import concourse.bass as bass
from concourse import mybir

B, D, T, NE = 1024, 1024, 4, 10
P = 128
HALVES, N = 2, 512
KT = D // P
NBT = N // P
EXPERTS = (8, 9, 0, 1, 2, 3, 4, 5, 6, 7)
DENSE = 16
TOP1, TOP2 = 512, 256
MT1, MT2 = TOP1 // P, TOP2 // P
STEP = 2 * KT
NG = T
LOGIT_ROWS = 66
ONES_ROW = 32

U_SH0, U_T0, U_SH1, U_DENSE = 0, STEP, STEP * (T + 1), STEP * (T + 2)
U_T1 = U_DENSE + 2
U_T1N = U_T1 + STEP
U_TAIL = U_T1N + (T - 1) * (STEP + MT1) + MT1
UNITS = U_TAIL + 2
EUNITS = 2 * STEP * (T + 1)
STEPS = 2 * (T + 1) + T + 1
GATED = 2 * T + 1
PAIRS = 8 * (T + 1) + 8 * T
BCASTS = 2 + 6 * T + 4 * T
GATE_LOADS = 16 + 32 * 2 * T
XBANKS = 2 * 5 * NBT
RAW = 4


def build(nc, ids, dense_t, tbl_0, tbl_1, tbl_2, tbl_3, tbl_4, w0, w1, w_top, w_dense, w_top2, w_top3,
          b0, b1, b_top1, b_top2, gs_w, g_w, g_b, comb_s, comb_t, gs_b, ident_in, out):
    f32, f32r, i32 = mybir.dt.float32, mybir.dt.float32r, mybir.dt.int32
    ALU, ACT, AX = mybir.AluOpType, mybir.ActivationFunctionType, mybir.AxisListType
    tables = (tbl_0, tbl_1, tbl_2, tbl_3, tbl_4)

    ctx = ExitStack()
    with ctx:
        def sb(name, shape, dt=f32):
            return ctx.enter_context(nc.sbuf_tensor(name, shape, dt))

        def bank(name):
            return ctx.enter_context(nc.psum_tensor(name, [P, N], f32))

        def sem(name):
            return ctx.enter_context(nc.semaphore(name))

        slots = sb("slots", [P, 5 * KT, N])
        act_hi = sb("act_hi", [P, KT, N], f32r)
        act_lo = sb("act_lo", [P, KT, N], f32r)
        eo_sh = sb("eo_sh", [P, 2 * KT, N])
        eo_b = sb("eo_b", [P, 4, N])
        raw = sb("raw", [P, RAW, KT * P])
        w_hi = sb("w_hi", [P, 2, KT * P], f32r)
        w_lo = sb("w_lo", [P, 2, KT * P], f32r)
        gate_b = sb("gate_b", [P, 6, N])
        prod = sb("prod", [P, 2, N])
        gw_raw = sb("gw_raw", [P, KT * NE])
        gw = sb("gw", [P, KT, LOGIT_ROWS], f32r)
        logit_t = sb("logit_t", [ONES_ROW + 1, N])
        gate_t = gw[0:12, :, :].rearrange("p k n -> p (k n)")[:, 0:N]
        comb_sh = sb("comb_sh", [ONES_ROW + 1, NE])
        comb_tk = sb("comb_tk", [ONES_ROW + 1, NG])
        lg = sb("lg", [P, NBT, NE])
        mx = sb("mx", [P, NBT])
        rs = sb("rs", [P, NBT])
        gsh = sb("gsh", [P, NBT, NE])
        g6 = sb("g6", [P, NBT, 6])
        g6r = sb("g6r", [P, NBT, 6], f32r)
        g12 = sb("g12", [P, NBT, 12])
        pick = sb("pick", [12, 6], f32r)
        ident = sb("ident", [P, P])
        idx = sb("idx", [P, 5 * HALVES * NBT], i32)
        bias0 = sb("bias0", [P, NE * KT])
        bias1 = sb("bias1", [P, NE * KT])
        bias_t1 = sb("bias_t1", [P, MT1])
        bias_t2 = sb("bias_t2", [P, MT2])
        w3 = sb("w3", [P, MT2])

        main = [bank(f"main{i}") for i in range(2)]
        gps = [bank(f"gps{i}") for i in range(2)]
        top = [bank(f"top{i}") for i in range(MT1)]

        consts_in = sem("consts_in")
        idx_in = sem("idx_in")
        raw_in = [sem(f"raw_in{i}") for i in range(RAW)]
        dctx_in = [sem(f"dctx_in{i}") for i in range(2)]
        gw_in = sem("gw_in")
        x_in = [sem(f"x_in{i}") for i in range(2)]
        y_out = sem("y_out")
        hi_split = sem("hi_split")
        lo_split = sem("lo_split")
        act_hi_rdy = sem("act_hi_rdy")
        act_lo_rdy = sem("act_lo_rdy")
        act_free = sem("act_free")
        unit_done = sem("unit_done")
        evac_done = sem("evac_done")
        xt_done = sem("xt_done")
        x_evac = sem("x_evac")
        pair_done = sem("pair_done")
        sh_done = sem("sh_done")
        gw_rdy = sem("gw_rdy")
        gw_step = sem("gw_step")
        logit_done = sem("logit_done")
        logit_evac = sem("logit_evac")
        lt_done = sem("lt_done")
        shift_rdy = sem("shift_rdy")
        exp_rdy = sem("exp_rdy")
        g12_rdy = sem("g12_rdy")
        gt_done = sem("gt_done")
        gt_evac = sem("gt_evac")
        bc_done = sem("bc_done")
        gb_rdy = sem("gb_rdy")
        chain = sem("chain")
        h1_rdy = sem("h1_rdy")
        t2_done = sem("t2_done")
        h2_rdy = sem("h2_rdy")
        y_done = sem("y_done")
        y_rdy = sem("y_rdy")
        pre_rdy = sem("pre_rdy")

        block = ctx.enter_context(nc.Block())

        def rows(g):
            return (4, g) if g < NBT else (g // NBT - 1, g % NBT)

        @block.sync
        def _(sp):
            def unit(src, i, slot, U, parts=P, cols=KT * P):
                if not isinstance(U, int) or U >= RAW:
                    sp.wait_ge(hi_split, U - RAW + 1)
                    sp.wait_ge(lo_split, U - RAW + 1)
                sp.dma_start(raw[0:parts, slot, 0:cols],
                             src[bass.ds(i, 1), 0:parts, :].rearrange("a p n -> p (a n)"))\
                    .then_inc(raw_in[slot], 16)

            def stream(src, first, count, U, off, start=0):
                with sp.Fori(start, count // RAW) as i:
                    for c in range(RAW):
                        unit(src, first + i * RAW + c, (off + c) % RAW, U + i * RAW + c)

            def gate_load(g, q):
                sp.wait_ge(gw_rdy, q)
                sp.wait_ge(lt_done, q)
                sp.dma_start(gw_raw[:, 0:KT * NG], g_w[bass.ds(g, 1), :, :].rearrange("a p n -> p (a n)"))\
                    .then_inc(gw_in, 16)
                sp.dma_start(comb_tk[ONES_ROW:ONES_ROW + 1, :], g_b[bass.ds(g, 1), :]).then_inc(gw_in, 16)

            def gated_stream(src, first, U, off, g, q, start=0):
                stream(src, first, STEP // 2, U, off, start)
                gate_load(g, q)
                stream(src, first + STEP // 2, STEP // 2, U + STEP // 2, off)

            sp.dma_start(idx[:, :], ids).then_inc(idx_in, 16)
            sp.dma_start(ident[:, :], ident_in).then_inc(consts_in, 16)
            for h in range(HALVES):
                base, gated = h * UNITS, h * GATED
                if h:
                    sp.wait_ge(gw_rdy, gated)
                sp.dma_start(gw_raw[:, :], gs_w).then_inc(gw_in, 16)
                if h == 0:
                    for c in range(RAW):
                        unit(w0, c, c, c)
                    for dst, src in ((bias0, b0), (bias1, b1), (bias_t1, b_top1), (bias_t2, b_top2), (w3, w_top3)):
                        sp.dma_start(dst[:, :], src).then_inc(consts_in, 16)
                    sp.dma_start(comb_sh[0:ONES_ROW, :], comb_s).then_inc(consts_in, 16)
                    sp.dma_start(comb_sh[ONES_ROW:ONES_ROW + 1, :], gs_b).then_inc(consts_in, 16)
                    sp.dma_start(comb_tk[0:ONES_ROW, :], comb_t).then_inc(consts_in, 16)
                gated_stream(w0, 0, base, 0, 0, gated + 1, start=1 if h == 0 else 0)
                with sp.Fori(0, T) as t:
                    gated_stream(w0, STEP + t * STEP, base + U_T0 + t * STEP, 0, t + 1, gated + 2 + t)
                stream(w1, 0, STEP, base + U_SH1, 0)
                for d in range(2):
                    slot = (U_DENSE + d) % RAW
                    unit(w_dense, d, slot, base + U_DENSE + d, parts=DENSE, cols=MT1 // 2 * P)
                    sp.dma_start(raw[0:DENSE, slot, N:2 * N], dense_t[:, h * N:(h + 1) * N])\
                        .then_inc(dctx_in[d], 16)
                off = U_T1 % RAW
                gated_stream(w1, STEP, base + U_T1, off, T + 1, gated + T + 2)
                with sp.Fori(0, T - 2) as t:
                    gated_stream(w1, 2 * STEP + t * STEP, base + U_T1N + t * (STEP + MT1), off, T + 2 + t,
                                 gated + T + 3 + t)
                    stream(w_top, t * MT1, MT1, base + U_T1N + STEP + t * (STEP + MT1), off)
                late = base + U_T1N + (T - 2) * (STEP + MT1)
                stream(w1, STEP * T, STEP, late, off)
                stream(w_top, (T - 2) * MT1, MT1, late + STEP, off)
                stream(w_top, (T - 1) * MT1, MT1, late + STEP + MT1, off)
                for d in range(2):
                    unit(w_top2, d, (U_TAIL + d) % RAW, base + U_TAIL + d, cols=2 * TOP2)
                sp.wait_ge(y_rdy, h + 1)
                sp.dma_start(out[h:h + 1, :], logit_t[0:1, :]).then_inc(y_out, 16)
            sp.wait_ge(y_out, 16 * HALVES)

        @block.gpsimd
        def _(pool):
            pool.wait_ge(idx_in, 16)
            for h in range(HALVES):
                if h:
                    pool.wait_ge(pair_done, h * PAIRS)
                for g in range(5 * NBT):
                    t, bt = rows(g)
                    if g >= 2:
                        pool.wait_ge(xt_done, h * XBANKS + 2 * (g - 1))
                    c = (t * HALVES + h) * NBT + bt
                    pool.indirect_dma_start(
                        eo_b[:, 2 * (g % 2):2 * (g % 2) + 2, :].rearrange("p a n -> p (a n)"), None,
                        tables[t], bass.IndirectOffsetOnAxis(ap=idx[:, c:c + 1], axis=0)).then_inc(x_in[g % 2], 16)

        @block.tensor
        def _(pe):
            def three(dst, lhs_hi, lhs_lo, rhs_hi, rhs_lo, start, stop):
                nc.tensor.matmul(dst, lhs_hi, rhs_hi, start=start, stop=False)
                nc.tensor.matmul(dst, lhs_hi, rhs_lo, start=False, stop=False)
                return nc.tensor.matmul(dst, lhs_lo, rhs_hi, start=False, stop=stop)

            def unit(dst, slot, U, S=None, last=False, start=True, stop=True, between=None):
                pe.wait_ge(hi_split, U + 1)
                pe.wait_ge(lo_split, U + 1)
                for k in range(KT):
                    if S is not None:
                        pe.wait_ge(act_hi_rdy, S * KT + k + 1)
                        pe.wait_ge(act_lo_rdy, S * KT + k + 1)
                    w = slice(k * P, (k + 1) * P)
                    mm = three(dst[:, :], w_hi[:, slot, w], w_lo[:, slot, w], act_hi[:, k, :], act_lo[:, k, :],
                               start and k == 0, stop and k == KT - 1)
                    if k == KT - 1:
                        mm.then_inc(unit_done, 1)
                    elif last:
                        mm.then_inc(act_free, 1)
                    if between:
                        between(k)

            def expert(u, U, E, **more):
                if not isinstance(E, int) or E >= 2:
                    pe.wait_ge(evac_done, E - 1)
                unit(main[u % 2], u % 2, U, **more)

            def logits(Q):
                def emit(k):
                    if k == 0:
                        pe.wait_ge(gw_rdy, Q + 1)
                        if not isinstance(Q, int) or Q:
                            pe.wait_ge(gt_evac, Q)
                    nc.tensor.matmul(gps[0][0:LOGIT_ROWS, :], gw[:, k, :], act_hi[:, k, :],
                                     start=(k == 0), stop=False, skip_group_check=True)
                    mm = nc.tensor.matmul(gps[0][0:LOGIT_ROWS, :], gw[:, k, :], act_lo[:, k, :],
                                          start=False, stop=(k == KT - 1), skip_group_check=True)
                    if k == KT - 1:
                        mm.then_inc(logit_done, 1)
                return emit

            def turn_logits(Q, R, shared):
                comb, n = (comb_sh, NE) if shared else (comb_tk, NG)

                def emit(k):
                    if k != 2:
                        return
                    pe.wait_ge(logit_evac, Q + 1)
                    pe.wait_ge(gw_in, shared if shared else gate_row(Q))
                    if not isinstance(R, int) or R:
                        pe.wait_ge(gb_rdy, R)
                    for bt in range(NBT):
                        mm = nc.tensor.matmul(gps[1][:, bt * n:(bt + 1) * n],
                                              logit_t[:, bt * P:(bt + 1) * P], comb[:, :], start=True, stop=True)
                    mm.then_inc(lt_done, 1)
                return emit

            def gate_row(Q):
                return gate_in_base[0] + Q * 32

            gate_in_base = [0]

            def turn_gates(Q):
                pe.wait_ge(g12_rdy, Q + 1)
                for bt in range(NBT):
                    mm = nc.tensor.matmul(gps[0][0:12, bt * P:(bt + 1) * P], g12[:, bt, :], ident[:, :],
                                          start=True, stop=True)
                mm.then_inc(gt_done, 1)

            def broadcast(Q, R, order, places):
                def emit(k):
                    for n in [i for i, at in enumerate(places) if at == k]:
                        if n == 0:
                            pe.wait_ge(gt_evac, Q + 1)
                        if n >= 2:
                            pe.wait_ge(gb_rdy, R + n - 1)
                        j = order[n]
                        nc.tensor.matmul(gps[1 - n % 2][:, :], pick[:, j:j + 1].broadcast_to([12, P]),
                                         gate_t, start=True, stop=True).then_inc(bc_done, 1)
                return emit

            def transposed(h, g, i=None):
                stage, add = g % 2, 0 if i is None else i
                pe.wait_ge(x_in[stage], 16 * (h * (5 * NBT // 2) + g // 2 + 1) + add * 16)
                for j in range(2):
                    x = h * XBANKS + 2 * g + j
                    if x >= 4:
                        pe.wait_ge(x_evac, x - 3 + add * 4)
                    for c in range(4):
                        k = 4 * j + c
                        mm = nc.tensor.transpose(
                            top[(2 * g + j) % 4][:, c * P:(c + 1) * P],
                            eo_b[:, 2 * stage + k // 4, (k % 4) * P:(k % 4 + 1) * P], ident[:, :])
                    mm.then_inc(xt_done, 1)

            def gated_step(U, E, S, Q, R, order, shared=0, x=None):
                def rows_after(u, i=None):
                    if x is not None:
                        transposed(x, NBT + u, i)

                n = len(order)
                spread = [4, 4, 6, 7][:n]
                expert(0, U, E, S=S, between=logits(Q))
                rows_after(0)
                expert(1, U + 1, E + 1, between=turn_logits(Q, R, shared))
                rows_after(1)
                bc = broadcast(Q, R, order, spread)

                def third(k):
                    if k == 0:
                        turn_gates(Q)
                    bc(k)

                expert(2, U + 2, E + 2, between=third)
                rows_after(2)
                expert(3, U + 3, E + 3, between=broadcast(Q, R, order, [-1] * 4 + [1, 3]) if n > 4 else None)
                rows_after(3)
                with pe.Fori(0, 5) as i:
                    for c in range(2):
                        expert(c, U + 4 + c + i * 2, E + 4 + c + i * 2)
                        rows_after(4 + c, i)
                expert(0, U + 14, E + 14)
                rows_after(14)
                expert(1, U + 15, E + 15, last=True)
                rows_after(15)

            def tower(U, S, stop=False):
                for m in range(MT1):
                    unit(top[m], m % 2, U + m, S=S if m == 0 else None, last=(m == MT1 - 1),
                         start=False, stop=stop)

            pe.wait_ge(pre_rdy, 1)
            for h in range(HALVES):
                u0, e0, s0, q0, r0 = h * UNITS, h * EUNITS, h * STEPS, h * GATED, h * BCASTS
                gate_in_base[0] = h * GATE_LOADS + 16 - q0 * 32
                for g in range(NBT):
                    transposed(h, g)
                gated_step(u0, e0, s0, q0, r0, [4, 5], shared=h * GATE_LOADS + 16, x=h)
                with pe.Fori(0, T) as t:
                    gated_step(u0 + U_T0 + t * STEP, e0 + STEP + t * STEP, s0 + 1 + t, q0 + 1 + t, r0 + 2 + t * 6,
                               [4, 0, 2, 3, 5, 1])
                u, e = u0 + U_SH1, e0 + (T + 1) * STEP
                expert(0, u, e, S=s0 + T + 1)
                expert(1, u + 1, e + 1)
                with pe.Fori(0, 6) as i:
                    for c in range(2):
                        expert(c, u + 2 + c + i * 2, e + 2 + c + i * 2)
                expert(0, u + 14, e + 14)
                expert(1, u + 15, e + 15, last=True)
                pe.wait_ge(x_evac, (h + 1) * XBANKS)
                for d in range(2):
                    U = u0 + U_DENSE + d
                    pe.wait_ge(hi_split, U + 1)
                    pe.wait_ge(lo_split, U + 1)
                    for c in range(2):
                        w = slice(c * P, (c + 1) * P)
                        mm = three(top[2 * d + c][:, :], w_hi[0:DENSE, d, w], w_lo[0:DENSE, d, w],
                                   w_hi[0:DENSE, d, N:2 * N], w_lo[0:DENSE, d, N:2 * N], True, False)
                    mm.then_inc(unit_done, 1)
                own = [0, 2, 3, 1]
                e, s, q, r = e + STEP, s0 + T + 2, q0 + T + 1, r0 + 2 + 6 * T
                gated_step(u0 + U_T1, e, s, q, r, own)
                e, s, q, r, u = e + STEP, s + 1, q + 1, r + 4, u0 + U_T1N
                with pe.Fori(0, T - 2) as t:
                    gated_step(u + t * (STEP + MT1), e + t * STEP, s + t * 2, q + t, r + t * 4, own)
                    tower(u + STEP + t * (STEP + MT1), s + 1 + t * 2)
                n = T - 2
                u, e, s, q, r = u + n * (STEP + MT1), e + n * STEP, s + 2 * n, q + n, r + 4 * n
                gated_step(u, e, s, q, r, own)
                tower(u + STEP, s + 1)
                tower(u + STEP + MT1, s + 2, stop=True)
                pe.wait_ge(evac_done, (h + 1) * EUNITS)
                for d in range(2):
                    U = u0 + U_TAIL + d
                    pe.wait_ge(hi_split, U + 1)
                    pe.wait_ge(lo_split, U + 1)
                    for c in range(2):
                        k = 2 * d + c
                        pe.wait_ge(act_hi_rdy, (s + 3) * KT + 2 * (k + 1))
                        pe.wait_ge(act_lo_rdy, (s + 3) * KT + 2 * (k + 1))
                        for m in range(MT2):
                            w = slice((c * MT2 + m) * P, (c * MT2 + m + 1) * P)
                            mm = three(main[m][:, :], w_hi[:, d, w], w_lo[:, d, w], act_hi[:, k, :], act_lo[:, k, :],
                                       k == 0, k == MT1 - 1)
                            if k == MT1 - 1 and m == 0:
                                mm.then_inc(t2_done, 1)
                    mm.then_inc(unit_done, 1)
                for k in range(MT2):
                    pe.wait_ge(h2_rdy, h * MT2 + k + 1)
                    mm = nc.tensor.matmul(gps[0][0:1, :], w3[:, k:k + 1], eo_sh[:, MT1 + k, :],
                                          start=(k == 0), stop=(k == MT2 - 1))
                    if k == 0:
                        mm.then_inc(act_free, KT - 1)
                mm.then_inc(y_done, 1)

        @block.scalar
        def _(act):
            def split_hi(U, slot, rawslot, turn, parts=P, free=True):
                act.wait_ge(raw_in[rawslot], 16 + 16 * turn if isinstance(turn, int) else turn * 16 + 16)
                if free:
                    act.wait_ge(unit_done, U - 1)
                nc.scalar.activation(w_hi[0:parts, slot, :], raw[0:parts, rawslot, :], ACT.Copy).then_inc(hi_split, 1)

            def evacuate(src, dst, bias):
                nc.scalar.activation(dst, src, ACT.Relu, bias=bias).then_inc(evac_done, 1)

            def hand_over(S, chunk, ks, U):
                for k in ks:
                    if not isinstance(S, int) or S:
                        if k < KT - 1:
                            act.wait_ge(act_free, (S - 1) * (KT - 1) + k + 1)
                        else:
                            act.wait_ge(unit_done, U)
                    nc.scalar.activation(act_hi[:, bass.ds(k, 1), :], slots[:, bass.ds(chunk + k, 1), :],
                                         ACT.Copy).then_inc(act_hi_rdy, 1)

            def rows_out(h, g):
                t, bt = rows(g)
                for j in range(2):
                    act.wait_ge(xt_done, h * XBANKS + 2 * g + j + 1)
                    nc.scalar.activation(
                        slots[:, t * KT + 4 * j:t * KT + 4 * j + 4, bt * P:(bt + 1) * P],
                        top[(2 * g + j) % 4][:, :].rearrange("p (k b) -> p k b", k=4), ACT.Copy).then_inc(x_evac, 1)

            def gate_copies(R, first, last, order):
                for n in range(first, last):
                    act.wait_ge(bc_done, R + n + 1)
                    nc.scalar.activation(gate_b[:, order[n], :], gps[1 - n % 2][:, :], ACT.Copy).then_inc(gb_rdy, 1)

            def gate_slot(j, Q, R, rows_, order, Pb):
                if j == 1:
                    act.wait_ge(logit_done, Q + 1)
                    if not isinstance(Q, int) or Q:
                        act.wait_ge(lt_done, Q)
                    nc.scalar.activation(logit_t[0:rows_, :], gps[0][0:rows_, :], ACT.Copy).then_inc(logit_evac, 1)
                    act.wait_ge(shift_rdy, Q + 1)
                    n = rows_ // 2
                    nc.scalar.activation(lg[:, :, 0:n], lg[:, :, 0:n], ACT.Exp).then_inc(exp_rdy, 1)
                if j == 2:
                    act.wait_ge(gt_done, Q + 1)
                    if not isinstance(R, int) or R:
                        act.wait_ge(bc_done, R)
                    nc.scalar.activation(gate_t, gps[0][0:12, :], ACT.Copy).then_inc(gt_evac, 1)
                    if not isinstance(Pb, int) or Pb:
                        act.wait_ge(pair_done, Pb)
                    gate_copies(R, 0, min(4, len(order)), order)
                if j == 3:
                    gate_copies(R, 4, len(order), order)

            def step(U, V, off, E, S, dest, bias, gates=None, x=None):
                for j in range(1, STEP - 1):
                    act.wait_ge(unit_done, U + j)
                    split_hi(U + j + 1, (j + 1) % 2, (off + j + 1) % RAW, V + (off + j + 1) // RAW, free=False)
                    dest_wait(dest, j - 1)
                    evacuate(main[(j - 1) % 2][:, :], dest(j - 1), bias(j - 1))
                    if x is not None:
                        rows_out(x, NBT + j - 1)
                    if gates:
                        gate_slot(j, *gates)

            def dest_wait(dest, u):
                if u in dest.waits:
                    for s_, v in dest.waits[u]:
                        act.wait_ge(s_, v)

            def shared_dest(waits):
                def dest(u):
                    return eo_sh[:, u, :]
                dest.waits = waits
                return dest

            def task_dest(t, S, Pb):
                def dest(u):
                    if u < KT:
                        return slots[:, bass.ds(t * KT + u, 1), :]
                    return eo_b[:, bass.ds(u % 4, 1), :]
                dest.waits = {
                    0: [(act_lo_rdy, (S + 1) * KT)],
                    KT: [(pair_done, Pb)],
                    KT + 4: [(pair_done, Pb + 5)],
                    KT + 6: [(pair_done, Pb + 6)],
                }
                return dest

            def biases(tile, first):
                return lambda u: tile[:, bass.ds(first + u, 1)]

            def change(U, V, off, dest, bias, S, chunk, x=None, shared=False):
                act.wait_ge(unit_done, U - 1)
                split_hi(U, 0, off % RAW, V, free=False)
                dest_wait(dest, STEP - 2)
                evacuate(main[0][:, :], dest(STEP - 2), bias(STEP - 2))
                if x is not None:
                    rows_out(x, NBT + STEP - 2)
                if shared:
                    for p in range(3):
                        act.wait_ge(sh_done, shared[0] + p)
                        hand_over(S, chunk, (2 * p, 2 * p + 1), U)
                else:
                    hand_over(S, chunk, range(KT), U)
                act.wait_ge(unit_done, U)
                dest_wait(dest, STEP - 1)
                evacuate(main[1][:, :], dest(STEP - 1), bias(STEP - 1))
                if x is not None:
                    rows_out(x, NBT + STEP - 1)
                if shared:
                    act.wait_ge(sh_done, shared[0] + 3)
                    hand_over(S, chunk, (6, 7), U)
                split_hi(U + 1, 1, (off + 1) % RAW, V + (off + 1) // RAW, free=False)

            def tower_slots(U, V, off, S, chunk, Un=None, next_units=True):
                for j in (1, 2):
                    act.wait_ge(unit_done, U + j)
                    split_hi(U + j + 1, (j + 1) % 2, (off + j + 1) % RAW, V + (off + j + 1) // RAW, free=False)
                act.wait_ge(unit_done, U + 3)
                split_hi(U + 4, 0, off, V + 1, free=False)
                if chunk is not None:
                    hand_over(S, chunk, range(KT), U + 4)
                act.wait_ge(unit_done, U + 4)
                split_hi(U + 5, 1, (off + 1) % RAW, V + 1 + (off + 1) // RAW, free=False)

            act.wait_ge(pre_rdy, 1)
            act.wait_ge(consts_in, 16 * 9)
            for h in range(HALVES):
                u0, e0, s0, q0, r0, p0 = h * UNITS, h * EUNITS, h * STEPS, h * GATED, h * BCASTS, h * PAIRS
                v0 = u0 // RAW
                split_hi(u0, 0, 0, v0, free=h > 0)
                split_hi(u0 + 1, 1, 1, v0, free=h > 0)
                if h:
                    act.wait_ge(act_lo_rdy, s0 * KT)
                for g in range(NBT):
                    rows_out(h, g)
                act.wait_ge(x_evac, h * XBANKS + 2 * NBT)
                if h:
                    act.wait_ge(y_done, h)
                hand_over(s0, 4 * KT, range(KT), u0)
                dest, bias = shared_dest({0: [(pair_done, p0)]} if h else {}), biases(bias0, 0)
                if h:
                    act.wait_ge(y_out, 16 * h)
                step(u0, v0, 0, e0, s0, dest, bias, (q0, r0, 2 * NE, [4, 5], p0), x=h)
                change(u0 + U_T0, v0 + U_T0 // RAW, 0, dest, bias, s0 + 1, 0, x=h)
                with act.Fori(0, T) as t:
                    U, V = u0 + U_T0 + t * STEP, v0 + U_T0 // RAW + t * (STEP // RAW)
                    S, Pb = s0 + 1 + t, p0 + 8 + t * 8
                    dest, bias = task_dest(t, S, Pb), biases(bias0, STEP + t * STEP)
                    step(U, V, 0, None, S, dest, bias, (q0 + 1 + t, r0 + 2 + t * 6, 2 * NG, [4, 0, 2, 3, 5, 1], Pb))
                    change(U + STEP, V + STEP // RAW, 0, dest, bias, S + 1, (t + 1) * KT,
                           shared=(h * 4 * T + 1 + t * 4,))
                U, V, S = u0 + U_SH1, v0 + U_SH1 // RAW, s0 + T + 1
                dest, bias = shared_dest({0: [(pair_done, p0 + 8 * T + 4)]}), biases(bias1, 0)
                step(U, V, 0, None, S, dest, bias)
                act.wait_ge(unit_done, U + STEP - 1)
                D0 = u0 + U_DENSE
                act.wait_ge(dctx_in[0], 16 * (h + 1))
                split_hi(D0, 0, 0, D0 // RAW, parts=DENSE, free=False)
                evacuate(main[0][:, :], dest(STEP - 2), bias(STEP - 2))
                hand_over(S + 1, 0, range(KT), U + STEP)
                act.wait_ge(unit_done, D0)
                act.wait_ge(dctx_in[1], 16 * (h + 1))
                split_hi(D0 + 1, 1, 1, D0 // RAW, parts=DENSE, free=False)
                evacuate(main[1][:, :], dest(STEP - 1), bias(STEP - 1))
                U, V, off = u0 + U_T1, (u0 + U_T1) // RAW, U_T1 % RAW
                act.wait_ge(unit_done, U - 1)
                split_hi(U, 0, off, V, free=False)
                act.wait_ge(unit_done, U)
                split_hi(U + 1, 1, off + 1, V, free=False)
                own = [0, 2, 3, 1]
                S, Pb, Q, R = S + 1, p0 + 8 * (T + 1), q0 + T + 1, r0 + 2 + 6 * T
                dest, bias = task_dest(0, S, Pb), biases(bias1, STEP)
                step(U, V, off, None, S, dest, bias, (Q, R, 2 * NG, own, Pb))
                change(U + STEP, V + STEP // RAW, off, dest, bias, S + 1, KT)
                Un, Vn = u0 + U_T1N, V + STEP // RAW
                both = STEP + MT1

                def task(t, n, Sn, Pn, Qn, Rn, Ut, Vt, last):
                    dest, bias = task_dest(t, Sn, Pn), biases(bias1, STEP + t * STEP)
                    step(Ut, Vt, off, None, Sn, dest, bias, (Qn, Rn, 2 * NG, own, Pn))
                    change(Ut + STEP, Vt + STEP // RAW, off, dest, bias, Sn + 1, (t - 1) * KT)
                    if last:
                        act.wait_ge(pair_done, Pn + 8)
                        tower_slots(Ut + STEP, Vt + STEP // RAW, off, Sn + 2, t * KT)
                    else:
                        tower_slots(Ut + STEP, Vt + STEP // RAW, off, Sn + 2, (t + 1) * KT)

                with act.Fori(0, T - 2) as n:
                    task(n + 1, n, S + 1 + n * 2, Pb + 8 + n * 8, Q + 1 + n, R + 4 + n * 4,
                         Un + n * both, Vn + n * (both // RAW), False)
                n = T - 2
                task(T - 1, n, S + 1 + n * 2, Pb + 8 + n * 8, Q + 1 + n, R + 4 + n * 4,
                     Un + n * both, Vn + n * (both // RAW), True)
                U, V = u0 + U_TAIL - MT1, (u0 + U_TAIL - MT1) // RAW
                tower_slots(U, V, off, None, None)
                s = s0 + STEPS - 1
                for m in range(MT1):
                    nc.scalar.activation(eo_sh[:, m, :], top[m][:, :], ACT.Relu, bias=bias_t1[:, m:m + 1])\
                        .then_inc(h1_rdy, 1)
                for m in range(MT1):
                    act.wait_ge(h1_rdy, h * MT1 + m + 1)
                    nc.scalar.activation(act_hi[:, m, :], eo_sh[:, m, :], ACT.Copy).then_inc(act_hi_rdy, 2)
                for m in range(MT2):
                    if m == 0:
                        act.wait_ge(t2_done, h + 1)
                    else:
                        act.wait_ge(unit_done, u0 + UNITS)
                    nc.scalar.activation(eo_sh[:, MT1 + m, :], main[m][:, :], ACT.Relu, bias=bias_t2[:, m:m + 1])\
                        .then_inc(h2_rdy, 1)
                act.wait_ge(y_done, h + 1)
                nc.scalar.activation(logit_t[0:1, :], gps[0][0:1, :], ACT.Copy).then_inc(y_rdy, 1)

        @block.vector
        def _(dve):
            class Count:
                start, n = 0, 0

            links = Count()

            def link(ins):
                links.n += 1
                ins.then_inc(chain, 1)
                dve.wait_ge(chain, links.start + links.n)

            def split_lo(U, slot, rawslot, turn, parts=P):
                dve.wait_ge(raw_in[rawslot], turn * 16 + 16)
                dve.wait_ge(hi_split, U + 1)
                nc.vector.tensor_tensor(w_lo[0:parts, slot, :], raw[0:parts, rawslot, :], w_hi[0:parts, slot, :],
                                        ALU.subtract).then_inc(lo_split, 1)

            def hand_over(S, chunk, ks):
                for k in ks:
                    dve.wait_ge(act_hi_rdy, S * KT + k + 1)
                    nc.vector.tensor_tensor(act_lo[:, bass.ds(k, 1), :], slots[:, bass.ds(chunk + k, 1), :],
                                            act_hi[:, bass.ds(k, 1), :], ALU.subtract).then_inc(act_lo_rdy, 1)

            def split_gates(q_in, Q, n, R):
                dve.wait_ge(gw_in, q_in)
                if not isinstance(Q, int) or Q:
                    dve.wait_ge(logit_done, Q)
                    dve.wait_ge(gb_rdy, R)
                src = gw_raw[:, 0:KT * n].rearrange("p (k n) -> p k n", k=KT)
                nc.vector.tensor_copy(gw[:, :, 0:n], src).then_inc(gw_step, 1)
                dve.wait_ge(gw_step, Q + 1)
                nc.vector.tensor_tensor(gw[:, :, n:2 * n], src, gw[:, :, 0:n], ALU.subtract).then_inc(gw_rdy, 1)

            def softmax(Q, n, shared_at=None):
                t = slice(0, n)
                dve.wait_ge(lt_done, Q + 1)
                ps = gps[1][:, 0:NBT * n].rearrange("p (b n) -> p b n", b=NBT)
                link(nc.vector.tensor_reduce(mx[:, :], ps, AX.X, ALU.max))
                nc.vector.tensor_tensor(lg[:, :, t], ps, mx[:, :, None].broadcast_to([P, NBT, n]),
                                        ALU.subtract).then_inc(shift_rdy, 1)
                dve.wait_ge(exp_rdy, Q + 1)
                link(nc.vector.tensor_reduce(mx[:, :], lg[:, :, t], AX.X, ALU.add))
                link(nc.vector.reciprocal(rs[:, :], mx[:, :]))
                inv = rs[:, :, None].broadcast_to([P, NBT, n])
                if n == NE:
                    link(nc.vector.tensor_tensor(gsh[:, :, :], lg[:, :, t], inv, ALU.mult))
                    link(nc.vector.tensor_copy(g6[:, :, 4:6], gsh[:, :, NE - 2:NE]))
                else:
                    link(nc.vector.tensor_tensor(g6[:, :, 0:n], lg[:, :, t], inv, ALU.mult))
                    if shared_at is not None:
                        link(nc.vector.tensor_copy(g6[:, :, 4:6], gsh[:, :, bass.ds(shared_at, 2)]))
                link(nc.vector.tensor_copy(g6r[:, :, :], g6[:, :, :]))
                link(nc.vector.tensor_copy(g12[:, :, 0:6], g6r[:, :, :]))
                nc.vector.tensor_tensor(g12[:, :, 6:12], g6[:, :, :], g6r[:, :, :], ALU.subtract).then_inc(g12_rdy, 1)

            def gate(j):
                return gate_b[:, j:j + 1, :].broadcast_to([P, 2, N])

            def mul(dst, src, j):
                link(nc.vector.tensor_tensor(dst, src, gate(j), ALU.mult))

            def add(dst, a, signal=None):
                ins = nc.vector.tensor_tensor(dst, dst, a, ALU.add)
                if signal is None:
                    link(ins)
                else:
                    ins.then_inc(signal[0], 1)
                    dve.wait_ge(*signal)

            def gating(kind, t, E, R, Pb, shb=None):
                def pair(first, p):
                    return slots[:, bass.ds(first * KT + 2 * p, 2), :]

                def sh(x, p):
                    return eo_sh[:, x * KT + 2 * p:x * KT + 2 * p + 2, :]

                tmp = prod[:, :, :]

                def ready(u, gates):
                    dve.wait_ge(evac_done, E + u + 2)
                    dve.wait_ge(gb_rdy, R + gates)

                def a_ops(p):
                    done = (pair_done, Pb + p + 1)
                    if kind == "shared":
                        return [lambda: (ready(2 * p, 1), nc.vector.tensor_tensor(
                            pair(4, p), sh(0, p), gate(4), ALU.mult).then_inc(pair_done, 1), dve.wait_ge(*done))]
                    a = pair(t, p)
                    own = [
                        lambda: mul(a, a, 0),
                        lambda: mul(tmp, sh(0, p), 2),
                        lambda: add(a, tmp),
                        lambda: mul(tmp, sh(1, p), 3),
                        lambda: add(a, tmp, done),
                    ]
                    if kind == "layer1":
                        return [lambda: (ready(2 * p, 3), own[0]())] + own[1:]
                    return [lambda: (ready(2 * p, 4), mul(tmp, a, 4)), lambda: add(pair(4, p), tmp)] + own

                def b_ops(p):
                    done = (pair_done, Pb + 5 + p)
                    if kind == "shared":
                        return [lambda: (ready(KT + 2 * p, 2), mul(tmp, sh(1, p), 5)),
                                lambda: add(pair(4, p), tmp, done)]
                    b = eo_b[:, 2 * (p % 2):2 * (p % 2) + 2, :]
                    own = [lambda: mul(b, b, 1), lambda: add(pair(t, p), b, done)]
                    if kind == "layer1":
                        return [lambda: (ready(KT + 2 * p, 4), own[0]()), own[1]]
                    return [lambda: (ready(KT + 2 * p, 6), mul(tmp, b, 5)),
                            lambda: add(pair(4, p), tmp, (sh_done, shb + p + 1))] + own

                return a_ops, b_ops

            def run(ops):
                for op in ops:
                    op()

            def step(U, V, off, ops=None, gates=None, split=None):
                for j in range(1, STEP - 1):
                    split_lo(U + j + 1, (j + 1) % 2, (off + j + 1) % RAW, V + (off + j + 1) // RAW)
                    if j == 1 and gates:
                        softmax(*gates)
                    if j == 8 and split:
                        split_gates(*split)
                    if ops and j >= 3:
                        a_ops, b_ops = ops
                        p, second = (j - 3) // 2, (j - 3) % 2
                        now = a_ops(p) if p < 4 else b_ops(p - 4)
                        cut = (len(now) + 1) // 2
                        run(now[cut:] if second else now[:cut])

            def change(U, V, off, S, chunk, ops, shared=False):
                split_lo(U, 0, off, V)
                b2, b3 = ops[1](2), ops[1](3)
                if shared:
                    hand_over(S, chunk, range(0, 4))
                    run(b2[:2])
                    hand_over(S, chunk, (4, 5))
                    run(b3[:2])
                    hand_over(S, chunk, (6, 7))
                    split_lo(U + 1, 1, off + 1, V)
                    run(b2[2:] + b3[2:])
                else:
                    hand_over(S, chunk, range(KT))
                    split_lo(U + 1, 1, off + 1, V)
                    run(b2 + b3)

            def tower_slots(U, V, off, S, chunk):
                for j in (1, 2):
                    split_lo(U + j + 1, (j + 1) % 2, (off + j + 1) % RAW, V + (off + j + 1) // RAW)
                split_lo(U + 4, 0, off, V + 1)
                if chunk is not None:
                    hand_over(S, chunk, range(KT))
                split_lo(U + 5, 1, (off + 1) % RAW, V + 1 + (off + 1) // RAW)

            def loop_links(i, per):
                begun = links.start + links.n
                links.start, links.n = begun + i * per, 0
                return begun

            def end_links(begun, turns, per):
                assert links.n == per, (links.n, per)
                links.start, links.n = begun + turns * per, 0

            nc.vector.memset(gw[:, :, :].bitcast(f32), 0.0).then_inc(chain, 1)
            nc.vector.memset(logit_t[:, :], 1.0).then_inc(chain, 1)
            nc.vector.memset(g6[:, :, :], 0.0).then_inc(chain, 1)
            links.n = 3
            dve.wait_ge(chain, 3)
            dve.wait_ge(consts_in, 16 * 9)
            link(nc.vector.tensor_tensor(pick[:, :], ident[0:12, 0:6], ident[0:12, 6:12], ALU.add))
            nc.vector.tensor_copy(prod[:, 0, 0:1], ident[:, 0:1]).then_inc(pre_rdy, 1)
            for h in range(HALVES):
                u0, e0, s0, q0, r0, p0 = h * UNITS, h * EUNITS, h * STEPS, h * GATED, h * BCASTS, h * PAIRS
                v0, gin = u0 // RAW, h * GATE_LOADS + 16
                split_gates(gin, q0, NE, r0)
                split_lo(u0, 0, 0, v0)
                split_lo(u0 + 1, 1, 1, v0)
                hand_over(s0, 4 * KT, range(KT))
                ops = gating("shared", 4, e0, r0, p0)
                step(u0, v0, 0, ops, (q0, NE), (gin + 32, q0 + 1, NG, r0 + 2))
                change(u0 + U_T0, v0 + U_T0 // RAW, 0, s0 + 1, 0, ops)
                with dve.Fori(0, T) as t:
                    per = LINKS_L0
                    begun = loop_links(t, per)
                    U, V = u0 + U_T0 + t * STEP, v0 + U_T0 // RAW + t * (STEP // RAW)
                    ops = gating("layer0", t, e0 + STEP + t * STEP, r0 + 2 + t * 6, p0 + 8 + t * 8,
                                 h * 4 * T + t * 4)
                    step(U, V, 0, ops, (q0 + 1 + t, NG, t * 2), (gin + 64 + t * 32, q0 + 2 + t, NG, r0 + 8 + t * 6))
                    change(U + STEP, V + STEP // RAW, 0, s0 + 2 + t, (t + 1) * KT, ops, shared=True)
                end_links(begun, T, per)
                U = u0 + U_SH1
                step(U, U // RAW, 0)
                D0, U, off = u0 + U_DENSE, u0 + U_T1, U_T1 % RAW
                V, S = U // RAW, s0 + T + 2
                dve.wait_ge(dctx_in[0], 16 * (h + 1))
                split_lo(D0, 0, 0, D0 // RAW, parts=DENSE)
                hand_over(S, 0, range(KT))
                dve.wait_ge(dctx_in[1], 16 * (h + 1))
                split_lo(D0 + 1, 1, 1, D0 // RAW, parts=DENSE)
                split_lo(U, 0, off, V)
                split_lo(U + 1, 1, off + 1, V)
                E, R, Pb, Q = e0 + (T + 2) * STEP, r0 + 2 + 6 * T, p0 + 8 * (T + 1), q0 + T + 1
                gin = gin + 32 * (T + 2)
                ops = gating("layer1", 0, E, R, Pb)
                step(U, V, off, ops, (Q, NG), (gin, Q + 1, NG, R + 4))
                change(U + STEP, V + STEP // RAW, off, S + 1, KT, ops)
                Un, Vn, both = U + STEP, V + STEP // RAW, STEP + MT1

                def task(t, n, Ut, Vt, last):
                    Sn, Pn = S + 1 + n * 2, Pb + 8 + n * 8
                    ops = gating("layer1", t, E + STEP + n * STEP, R + 4 + n * 4, Pn)
                    split = None if last else (gin + 32 + n * 32, Q + 2 + n, NG, R + 8 + n * 4)
                    step(Ut, Vt, off, ops, (Q + 1 + n, NG), split)
                    change(Ut + STEP, Vt + STEP // RAW, off, Sn + 1, (t - 1) * KT, ops)
                    tower_slots(Ut + STEP, Vt + STEP // RAW, off, Sn + 2, t * KT if last else (t + 1) * KT)

                with dve.Fori(0, T - 2) as n:
                    per = LINKS_L1
                    begun = loop_links(n, per)
                    task(n + 1, n, Un + n * both, Vn + n * (both // RAW), False)
                end_links(begun, T - 2, per)
                n = T - 2
                task(T - 1, n, Un + n * both, Vn + n * (both // RAW), True)
                U = u0 + U_TAIL - MT1
                tower_slots(U, U // RAW, off, None, None)
                s = s0 + STEPS - 1
                for m in range(MT1):
                    dve.wait_ge(act_hi_rdy, s * KT + 2 * (m + 1))
                    nc.vector.tensor_tensor(act_lo[:, m, :], eo_sh[:, m, :], act_hi[:, m, :], ALU.subtract)\
                        .then_inc(act_lo_rdy, 2)


LINKS_L0 = 7 + 4 * 6 + 4 * 2
LINKS_L1 = 6 + 4 * 4 + 4 * 1


def _units(w, strips):
    e, k, _ = w.shape
    return np.ascontiguousarray(
        w.reshape(e, k // P, P, strips, P).transpose(0, 3, 2, 1, 4).reshape(e * strips, P, k))


def kernel(dense_ctx, ids, tbl_0, tbl_1, tbl_2, tbl_3, tbl_4, W_top1, b_top1, W_top2, b_top2, W_top3,
           L0_rec_W0, L0_rec_b0, L0_rec_G0w, L0_rec_G0b, L0_rec_Gs0w, L0_rec_Gs0b, L0_rec_W1, L0_rec_b1,
           L0_rec_G1w, L0_rec_G1b):
    import concourse.bacc as bacc
    from concourse.bass_utils import run_bass_kernel_spmd as run

    a = {k: np.asarray(v) for k, v in locals().items() if k not in ("bacc", "run")}
    order = list(EXPERTS)

    def kt_cols(w):
        k, n = w.shape
        return np.ascontiguousarray(w.reshape(k // P, P, n).transpose(1, 0, 2).reshape(P, -1))

    def per_part(v):
        return np.ascontiguousarray(v.reshape(-1, P).T)

    def combine(n):
        c = np.zeros((ONES_ROW, n), np.float32)
        c[np.arange(2 * n), np.arange(2 * n) % n] = 1.0
        return c

    w_top1 = a["W_top1"]
    laid = {
        "ids": np.ascontiguousarray(a["ids"].T.reshape(5 * HALVES * NBT, P).T),
        "dense_t": np.ascontiguousarray(a["dense_ctx"].T),
        "tbl_0": a["tbl_0"], "tbl_1": a["tbl_1"], "tbl_2": a["tbl_2"], "tbl_3": a["tbl_3"], "tbl_4": a["tbl_4"],
        "w0": _units(a["L0_rec_W0"][order], KT),
        "w1": _units(a["L0_rec_W1"][order], KT),
        "w_top": _units(w_top1[:T * D].reshape(T, D, TOP1), MT1),
        "w_dense": np.ascontiguousarray(w_top1[T * D:].reshape(DENSE, 2, TOP1 // 2).transpose(1, 0, 2)),
        "w_top2": np.ascontiguousarray(
            a["W_top2"].reshape(2, 2, P, TOP2).transpose(0, 2, 1, 3).reshape(2, P, 2 * TOP2)),
        "w_top3": per_part(a["W_top3"]),
        "b0": per_part(a["L0_rec_b0"][order]), "b1": per_part(a["L0_rec_b1"][order]),
        "b_top1": per_part(a["b_top1"]), "b_top2": per_part(a["b_top2"]),
        "gs_w": kt_cols(a["L0_rec_Gs0w"]),
        "g_w": np.stack([kt_cols(w) for w in (*a["L0_rec_G0w"], *a["L0_rec_G1w"])]),
        "g_b": np.concatenate([a["L0_rec_G0b"], a["L0_rec_G1b"]]),
        "comb_s": combine(NE), "comb_t": combine(NG),
        "gs_b": a["L0_rec_Gs0b"].reshape(1, NE),
        "ident_in": np.eye(P, dtype=np.float32),
    }
    nc = bacc.Bacc("TRN2", target_bir_lowering=False, num_devices=1)
    args = {n: nc.dram_tensor(f"in_{n}", v.shape, mybir.dt.from_np(v.dtype), kind="ExternalInput").ap()
            for n, v in laid.items()}
    y = nc.dram_tensor("y", (HALVES, N), mybir.dt.float32, kind="ExternalOutput").ap()
    build(nc, out=y, **args)
    r = run(nc, [{f"in_{n}": v for n, v in laid.items()}], core_ids=[0])
    return np.asarray(r.results[0]["y"]).reshape(B, 1)
```

```python
from contextlib import ExitStack

import numpy as np
import concourse.bass as bass
from concourse import mybir

B, D, T, NE = 1024, 1024, 4, 10
P = 128
HALVES, N = 2, 512
KT = D // P
NBT = N // P
EXPERTS = (8, 9, 0, 1, 2, 3, 4, 5, 6, 7)
DENSE = 16
TOP1, TOP2 = 512, 256
MT1, MT2 = TOP1 // P, TOP2 // P
STEP = 2 * KT
NG = T
LOGIT_ROWS = 66
ONES_ROW = 32

U_SH0, U_T0, U_SH1, U_DENSE = 0, STEP, STEP * (T + 1), STEP * (T + 2)
U_T1 = U_DENSE + 2
U_T1N = U_T1 + STEP
HALF_UNITS = U_T1N + (T - 1) * (STEP + MT1) + MT1
EUNITS = 2 * STEP * (T + 1)
HALF_STEPS = 2 * (T + 1) + T
GATED = 2 * T + 1
PAIRS = 8 * (T + 1) + 8 * T
BCASTS = 2 + 6 * T + 4 * T
GATE_LOADS = 16 + 32 * 2 * T
DENSE_COLS = TOP1 // 2 + N
XBANKS = 2 * 5 * NBT
RAW = 4


def build(nc, ids, dense_t, tbl_0, tbl_1, tbl_2, tbl_3, tbl_4, w0, w1, w_top, w_dense, w_top2, w_top3,
          b0, b1, b_top1, b_top2, gs_w, g_w, g_b, comb_s, comb_t, gs_b, ident_in, out):
    f32, f32r, i32 = mybir.dt.float32, mybir.dt.float32r, mybir.dt.int32
    ALU, ACT, AX = mybir.AluOpType, mybir.ActivationFunctionType, mybir.AxisListType
    tables = (tbl_0, tbl_1, tbl_2, tbl_3, tbl_4)

    ctx = ExitStack()
    with ctx:
        def sb(name, shape, dt=f32):
            return ctx.enter_context(nc.sbuf_tensor(name, shape, dt))

        def bank(name):
            return ctx.enter_context(nc.psum_tensor(name, [P, N], f32))

        def sem(name):
            return ctx.enter_context(nc.semaphore(name))

        slots = sb("slots", [P, 5 * KT, N])
        act_hi = sb("act_hi", [P, KT, N], f32r)
        act_lo = sb("act_lo", [P, KT, N], f32r)
        eo_sh = sb("eo_sh", [P, 2 * KT, N])
        eo_b = sb("eo_b", [P, 4, N])
        raw = sb("raw", [P, RAW, KT * P])
        w_hi = sb("w_hi", [P, 2, KT * P], f32r)
        w_lo = sb("w_lo", [P, 2, KT * P], f32r)
        gate_b = sb("gate_b", [P, 6, N])
        prod = sb("prod", [P, 2, N])
        gw_raw = sb("gw_raw", [P, KT * NE])
        gw = sb("gw", [P, KT, LOGIT_ROWS], f32r)
        logit_t = sb("logit_t", [ONES_ROW + 1, N])
        gate_t = gw[0:12, :, :].rearrange("p k n -> p (k n)")[:, 0:N]
        comb = sb("comb", [ONES_ROW + 1, NE + NG])
        comb_sh, comb_tk = comb[:, 0:NE], comb[:, NE:]
        lg = sb("lg", [P, NBT, NE])
        small = sb("small", [P, 2 * NBT + 2])
        mx, rs, warm = small[:, 0:NBT], small[:, NBT:2 * NBT], small[:, 2 * NBT:]
        gsh = sb("gsh", [P, NBT, NE])
        g6 = sb("g6", [P, NBT, 6])
        g12 = sb("g12", [P, NBT, LOGIT_ROWS], f32r)
        pick = sb("pick", [12, 6], f32r)
        ident = sb("ident", [P, P])
        ident_r = sb("ident_r", [P, P], f32r)
        idx = sb("idx", [P, 5 * HALVES * NBT], i32)
        bias0 = sb("bias0", [P, NE * KT])
        bias1 = sb("bias1", [P, NE * KT])
        tower_c = sb("tower_c", [P, MT1 + 2 * MT2])
        bias_t1, bias_t2, w3 = tower_c[:, 0:MT1], tower_c[:, MT1:MT1 + MT2], tower_c[:, MT1 + MT2:]

        main = [bank(f"main{i}") for i in range(2)]
        gps = [bank(f"gps{i}") for i in range(2)]
        top = [bank(f"top{i}") for i in range(MT1)]

        consts_in = sem("consts_in")
        idx_in = sem("idx_in")
        raw_in = [sem(f"raw_in{i}") for i in range(RAW)]
        dctx_in = [sem(f"dctx_in{i}") for i in range(2)]
        gw_in = sem("gw_in")
        ident_rdy = sem("ident_rdy")
        x_in = [sem(f"x_in{i}") for i in range(2)]
        x0_in = [sem(f"x0_in{i}") for i in range(NBT)]
        y_out = sem("y_out")
        hi_split = sem("hi_split")
        lo_split = sem("lo_split")
        act_hi_rdy = sem("act_hi_rdy")
        act_lo_rdy = sem("act_lo_rdy")
        act_free = sem("act_free")
        unit_done = sem("unit_done")
        evac_done = sem("evac_done")
        xt_done = sem("xt_done")
        x_evac = sem("x_evac")
        pair_done = sem("pair_done")
        sh_done = sem("sh_done")
        gw_rdy = sem("gw_rdy")
        gw_step = sem("gw_step")
        logit_done = sem("logit_done")
        logit_evac = sem("logit_evac")
        lt_done = sem("lt_done")
        shift_rdy = sem("shift_rdy")
        exp_rdy = sem("exp_rdy")
        g12_rdy = sem("g12_rdy")
        gt_done = sem("gt_done")
        gt_evac = sem("gt_evac")
        bc_done = sem("bc_done")
        gb_rdy = sem("gb_rdy")
        chain = sem("chain")
        h1_rdy = sem("h1_rdy")
        t2_done = sem("t2_done")
        h2_rdy = sem("h2_rdy")
        y_done = sem("y_done")
        y_rdy = sem("y_rdy")
        pre_rdy = sem("pre_rdy")

        block = ctx.enter_context(nc.Block())

        def rows(g):
            return (4, g) if g < NBT else (g // NBT - 1, g % NBT)

        def staged(h, g):
            first = h == 0 and g < NBT
            tile, at = (slots, 2 * g) if first else (eo_b, 2 * (g % 2))
            return tile[:, at:at + 2, :].rearrange("p a (k c) -> p (a k) c", c=P)

        def arrival(h, g):
            if h == 0 and g < NBT:
                return x0_in[g], 16
            before = h * (5 * NBT - NBT) // 2 + g // 2 - (NBT // 2 if h == 0 else 0)
            return x_in[g % 2], 16 * (before + 1)

        def xbank(g, j):
            return (main + gps if g < NBT else top)[(2 * g + j) % 4]

        def places(h):
            return h * HALF_UNITS, h * (HALF_UNITS + 2)

        def steps(h):
            return h * HALF_STEPS, h * (HALF_STEPS + 1)

        @block.sync
        def _(sp):
            def unit(src, i, slot, U, parts=P, cols=KT * P):
                if not isinstance(U, int) or U >= RAW:
                    sp.wait_ge(hi_split, U - RAW + 1)
                    sp.wait_ge(lo_split, U - RAW + 1)
                sp.dma_start(raw[0:parts, slot, 0:cols],
                             src[bass.ds(i, 1), 0:parts, :].rearrange("a p n -> p (a n)"))\
                    .then_inc(raw_in[slot], 16)

            def stream(src, first, count, U, off, start=0):
                with sp.Fori(start, count // RAW) as i:
                    for c in range(RAW):
                        unit(src, first + i * RAW + c, (off + c) % RAW, U + i * RAW + c)

            def gate_load(g, q):
                sp.wait_ge(gw_rdy, q)
                sp.wait_ge(lt_done, q)
                sp.dma_start(gw_raw[:, 0:KT * NG], g_w[bass.ds(g, 1), :, :].rearrange("a p n -> p (a n)"))\
                    .then_inc(gw_in, 16)
                sp.dma_start(comb_tk[ONES_ROW:ONES_ROW + 1, :], g_b[bass.ds(g, 1), :]).then_inc(gw_in, 16)

            def top2(h, U):
                for d in range(2):
                    unit(w_top2, d, (U + d) % RAW, U + d, cols=2 * TOP2)

            def gated_stream(src, first, U, off, g, q, start=0):
                stream(src, first, STEP // 2, U, off, start)
                gate_load(g, q)
                stream(src, first + STEP // 2, STEP // 2, U + STEP // 2, off)

            sp.dma_start(idx[:, :], ids).then_inc(idx_in, 16)
            sp.dma_start(ident[:, :], ident_in).then_inc(ident_rdy, 16)
            sp.dma_start(gw_raw[:, :], gs_w).then_inc(gw_in, 16)
            for h in range(HALVES):
                (first, base), gated = places(h), h * GATED
                if h == 0:
                    for c in range(RAW):
                        unit(w0, c, c, c)
                gated_stream(w0, 0, first, first % RAW, 0, gated + 1, start=1 if h == 0 else 0)
                if h:
                    top2(h - 1, first + STEP)
                with sp.Fori(0, T) as t:
                    gated_stream(w0, STEP + t * STEP, base + U_T0 + t * STEP, 0, t + 1, gated + 2 + t)
                stream(w1, 0, STEP, base + U_SH1, 0)
                for d in range(2):
                    slot = (U_DENSE + d) % RAW
                    unit(w_dense, d, slot, base + U_DENSE + d, parts=DENSE, cols=TOP1 // 2)
                    sp.dma_start(raw[0:DENSE, slot, TOP1 // 2:DENSE_COLS], dense_t[:, h * N:(h + 1) * N])\
                        .then_inc(dctx_in[d], 16)
                off = U_T1 % RAW
                gated_stream(w1, STEP, base + U_T1, off, T + 1, gated + T + 2)
                with sp.Fori(0, T - 2) as t:
                    gated_stream(w1, 2 * STEP + t * STEP, base + U_T1N + t * (STEP + MT1), off, T + 2 + t,
                                 gated + T + 3 + t)
                    stream(w_top, t * MT1, MT1, base + U_T1N + STEP + t * (STEP + MT1), off)
                late = base + U_T1N + (T - 2) * (STEP + MT1)
                stream(w1, STEP * T, STEP // 2, late, off)
                if h + 1 < HALVES:
                    sp.wait_ge(gw_rdy, gated + GATED)
                    sp.dma_start(gw_raw[:, :], gs_w).then_inc(gw_in, 16)
                stream(w1, STEP * T + STEP // 2, STEP // 2, late + STEP // 2, off)
                stream(w_top, (T - 2) * MT1, MT1, late + STEP, off)
                stream(w_top, (T - 1) * MT1, MT1, late + STEP + MT1, off)
            top2(HALVES - 1, late + STEP + 2 * MT1)

        @block.gpsimd
        def _(pool):
            pool.wait_ge(idx_in, 16)
            for h in range(HALVES):
                if h:
                    pool.wait_ge(pair_done, h * PAIRS)
                for g in range(5 * NBT):
                    t, bt = rows(g)
                    if g >= (NBT + 2 if h == 0 else 2):
                        pool.wait_ge(xt_done, h * XBANKS + 2 * (g - 1))
                    c = (t * HALVES + h) * NBT + bt
                    pool.indirect_dma_start(
                        staged(h, g).rearrange("p k c -> p (k c)"), None,
                        tables[t], bass.IndirectOffsetOnAxis(ap=idx[:, c:c + 1], axis=0))\
                        .then_inc(arrival(h, g)[0], 16)

        @block.tensor
        def _(pe):
            def three(dst, lhs_hi, lhs_lo, rhs_hi, rhs_lo, start, stop):
                nc.tensor.matmul(dst, lhs_hi, rhs_hi, start=start, stop=False)
                nc.tensor.matmul(dst, lhs_hi, rhs_lo, start=False, stop=False)
                return nc.tensor.matmul(dst, lhs_lo, rhs_hi, start=False, stop=stop)

            def unit(dst, slot, U, S=None, last=False, start=True, stop=True, between=None):
                pe.wait_ge(hi_split, U + 1)
                pe.wait_ge(lo_split, U + 1)
                for k in range(KT):
                    if S is not None:
                        pe.wait_ge(act_hi_rdy, S * KT + k + 1)
                        pe.wait_ge(act_lo_rdy, S * KT + k + 1)
                    w = slice(k * P, (k + 1) * P)
                    mm = three(dst[:, :], w_hi[:, slot, w], w_lo[:, slot, w], act_hi[:, k, :], act_lo[:, k, :],
                               start and k == 0, stop and k == KT - 1)
                    if k == KT - 1:
                        mm.then_inc(unit_done, 1)
                    elif last:
                        mm.then_inc(act_free, 1)
                    if between:
                        between(k)

            def expert(u, U, E, **more):
                if not isinstance(E, int) or E >= 2:
                    pe.wait_ge(evac_done, E - 1)
                unit(main[u % 2], u % 2, U, **more)

            def logits(Q):
                def emit(k):
                    if k == 0:
                        pe.wait_ge(gw_rdy, Q + 1)
                        if not isinstance(Q, int) or Q:
                            pe.wait_ge(gt_evac, Q)
                    nc.tensor.matmul(gps[0][0:LOGIT_ROWS, :], gw[:, k, :], act_hi[:, k, :],
                                     start=(k == 0), stop=False, skip_group_check=True)
                    mm = nc.tensor.matmul(gps[0][0:LOGIT_ROWS, :], gw[:, k, :], act_lo[:, k, :],
                                          start=False, stop=(k == KT - 1), skip_group_check=True)
                    if k == KT - 1:
                        mm.then_inc(logit_done, 1)
                return emit

            def turn_logits(Q, R, shared):
                adder, n = (comb_sh, NE) if shared else (comb_tk, NG)

                def emit(k):
                    if k != 3:
                        return
                    pe.wait_ge(logit_evac, Q + 1)
                    pe.wait_ge(gw_in, shared if shared else gate_row(Q))
                    if not isinstance(R, int) or R:
                        pe.wait_ge(gb_rdy, R)
                    for bt in range(NBT):
                        mm = nc.tensor.matmul(gps[1][:, bt * n:(bt + 1) * n],
                                              logit_t[:, bt * P:(bt + 1) * P], adder, start=True, stop=True)
                    mm.then_inc(lt_done, 1)
                return emit

            def gate_row(Q):
                return gate_in_base[0] + Q * 32

            gate_in_base = [0]

            def turn_gates(Q):
                pe.wait_ge(g12_rdy, Q + 1)
                for bt in range(NBT):
                    mm = nc.tensor.matmul(gps[0][0:LOGIT_ROWS, bt * P:(bt + 1) * P], g12[:, bt, :], ident_r[:, :],
                                          start=True, stop=True)
                mm.then_inc(gt_done, 1)

            def broadcast(Q, R, order, places):
                def emit(k):
                    for n in [i for i, at in enumerate(places) if at == k]:
                        if n == 0:
                            pe.wait_ge(gt_evac, Q + 1)
                        if n >= 2:
                            pe.wait_ge(gb_rdy, R + n - 1)
                        j = order[n]
                        nc.tensor.matmul(gps[1 - n % 2][:, :], pick[:, j:j + 1].broadcast_to([12, P]),
                                         gate_t, start=True, stop=True).then_inc(bc_done, 1)
                return emit

            def transposed(h, g, i=None):
                add = 0 if i is None else i
                where, count = arrival(h, g)
                pe.wait_ge(where, count + add * 16)
                for j in range(2):
                    x = h * XBANKS + 2 * g + j
                    if x >= 4:
                        pe.wait_ge(x_evac, x - 3 + add * 4)
                    for c in range(4):
                        mm = nc.tensor.transpose(xbank(g, j)[:, c * P:(c + 1) * P],
                                                 staged(h, g)[:, 4 * j + c, :], ident[:, :])
                    mm.then_inc(xt_done, 1)

            def gated_step(U, E, S, Q, R, order, shared=0, x=None):
                def rows_after(u, i=None):
                    if x and u == 0:
                        pe.wait_ge(h1_rdy, x * MT1)
                    if x is not None:
                        transposed(x, NBT + u, i)

                n = len(order)
                spread = [4, 4, 6, 7][:n] if n != 4 else [4, 4, 6, -1]
                expert(0, U, E, S=S, between=logits(Q))
                rows_after(0)
                expert(1, U + 1, E + 1, between=turn_logits(Q, R, shared))
                rows_after(1)
                bc = broadcast(Q, R, order, spread)

                def third(k):
                    if k == 1:
                        turn_gates(Q)
                    bc(k)

                expert(2, U + 2, E + 2, between=third)
                rows_after(2)
                expert(3, U + 3, E + 3, between=broadcast(Q, R, order, [-1] * 4 + [1, 3] if n > 4 else [-1] * 3 + [1])
                       if n > 2 else None)
                rows_after(3)
                with pe.Fori(0, 5) as i:
                    for c in range(2):
                        expert(c, U + 4 + c + i * 2, E + 4 + c + i * 2)
                        rows_after(4 + c, i)
                expert(0, U + 14, E + 14)
                rows_after(14)
                expert(1, U + 15, E + 15, last=True)
                rows_after(15)

            def tower(U, S, stop=False, h_next=None):
                for m in range(MT1):
                    if h_next is not None and m:
                        if m == 1:
                            pe.wait_ge(evac_done, h_next * EUNITS)
                            pe.wait_ge(gb_rdy, h_next * BCASTS)
                        for g in ((0, 1), (2,), (3,))[m - 1]:
                            transposed(h_next, g)
                    unit(top[m], m % 2, U + m, S=S if m == 0 else None, last=(m == MT1 - 1),
                         start=False, stop=stop)

            def tower2(h, U, S, banks):
                for d in range(2):
                    pe.wait_ge(hi_split, U + d + 1)
                    pe.wait_ge(lo_split, U + d + 1)
                    for c in range(2):
                        k = 2 * d + c
                        pe.wait_ge(act_hi_rdy, S * KT + 2 * (k + 1))
                        pe.wait_ge(act_lo_rdy, S * KT + 2 * (k + 1))
                        for m in range(MT2):
                            w = slice((c * MT2 + m) * P, (c * MT2 + m + 1) * P)
                            mm = three(banks[m][:, :], w_hi[:, d, w], w_lo[:, d, w], act_hi[:, k, :], act_lo[:, k, :],
                                       k == 0, k == MT1 - 1)
                            if k == MT1 - 1 and m == 0:
                                mm.then_inc(t2_done, 1)
                    mm.then_inc(unit_done, 1)
                for k in range(MT2):
                    pe.wait_ge(h2_rdy, h * MT2 + k + 1)
                    mm = nc.tensor.matmul(banks[2][0:1, :], w3[:, k:k + 1], eo_b[:, k, :],
                                          start=(k == 0), stop=(k == MT2 - 1))
                    if k == 0:
                        mm.then_inc(act_free, KT - 1)
                mm.then_inc(y_done, 1)

            pe.wait_ge(ident_rdy, 16)
            for g in range(NBT):
                transposed(0, g)
            pe.wait_ge(pre_rdy, 1)
            for h in range(HALVES):
                (first, u0), (sf, s0), e0, q0, r0 = places(h), steps(h), h * EUNITS, h * GATED, h * BCASTS
                gate_in_base[0] = h * GATE_LOADS + 16 - q0 * 32
                pe.wait_ge(x_evac, h * XBANKS + 2 * NBT)
                gated_step(first, e0, sf, q0, r0, [4, 5], shared=h * GATE_LOADS + 16, x=h)
                if h:
                    pe.wait_ge(x_evac, h * XBANKS + XBANKS)
                    tower2(h - 1, first + STEP, s0, top)
                with pe.Fori(0, T) as t:
                    gated_step(u0 + U_T0 + t * STEP, e0 + STEP + t * STEP, s0 + 1 + t, q0 + 1 + t, r0 + 2 + t * 6,
                               [4, 0, 2, 3, 5, 1])
                u, e = u0 + U_SH1, e0 + (T + 1) * STEP
                expert(0, u, e, S=s0 + T + 1)
                expert(1, u + 1, e + 1)
                with pe.Fori(0, 6) as i:
                    for c in range(2):
                        expert(c, u + 2 + c + i * 2, e + 2 + c + i * 2)
                expert(0, u + 14, e + 14)
                expert(1, u + 15, e + 15, last=True)
                pe.wait_ge(x_evac, (h + 1) * XBANKS)
                if h:
                    pe.wait_ge(y_rdy, h)
                for d in range(2):
                    U = u0 + U_DENSE + d
                    pe.wait_ge(hi_split, U + 1)
                    pe.wait_ge(lo_split, U + 1)
                    for c in range(2):
                        w = slice(c * P, (c + 1) * P)
                        mm = three(top[2 * d + c][:, :], w_hi[0:DENSE, d, w], w_lo[0:DENSE, d, w],
                                   w_hi[0:DENSE, d, TOP1 // 2:DENSE_COLS], w_lo[0:DENSE, d, TOP1 // 2:DENSE_COLS], True, False)
                    mm.then_inc(unit_done, 1)
                own = [0, 2, 3, 1]
                e, s, q, r = e + STEP, s0 + T + 2, q0 + T + 1, r0 + 2 + 6 * T
                gated_step(u0 + U_T1, e, s, q, r, own)
                e, s, q, r, u = e + STEP, s + 1, q + 1, r + 4, u0 + U_T1N
                with pe.Fori(0, T - 2) as t:
                    gated_step(u + t * (STEP + MT1), e + t * STEP, s + t * 2, q + t, r + t * 4, own)
                    tower(u + STEP + t * (STEP + MT1), s + 1 + t * 2)
                n = T - 2
                u, e, s, q, r = u + n * (STEP + MT1), e + n * STEP, s + 2 * n, q + n, r + 4 * n
                gated_step(u, e, s, q, r, own)
                tower(u + STEP, s + 1)
                tower(u + STEP + MT1, s + 2, stop=True, h_next=h + 1 if h + 1 < HALVES else None)
            pe.wait_ge(evac_done, HALVES * EUNITS)
            tower2(HALVES - 1, u + STEP + 2 * MT1, s + 3, main + gps)

        @block.scalar
        def _(act):
            def split_hi(slot, rawslot, turn, parts=P, cols=KT * P):
                act.wait_ge(raw_in[rawslot], turn * 16 + 16)
                nc.scalar.activation(w_hi[0:parts, slot, 0:cols], raw[0:parts, rawslot, 0:cols], ACT.Copy)\
                    .then_inc(hi_split, 1)

            def evacuate(src, dst, bias):
                nc.scalar.activation(dst, src, ACT.Relu, bias=bias).then_inc(evac_done, 1)

            def hand_over(S, chunk, ks, U):
                for k in ks:
                    if not isinstance(S, int) or S:
                        if k < KT - 1:
                            act.wait_ge(act_free, (S - 1) * (KT - 1) + k + 1)
                        else:
                            act.wait_ge(unit_done, U)
                    nc.scalar.activation(act_hi[:, bass.ds(k, 1), :], slots[:, bass.ds(chunk + k, 1), :],
                                         ACT.Copy).then_inc(act_hi_rdy, 1)

            def rows_out(h, g):
                t, bt = rows(g)
                for j in range(2):
                    act.wait_ge(xt_done, h * XBANKS + 2 * g + j + 1)
                    nc.scalar.activation(
                        slots[:, t * KT + 4 * j:t * KT + 4 * j + 4, bt * P:(bt + 1) * P],
                        xbank(g, j)[:, :].rearrange("p (k b) -> p k b", k=4), ACT.Copy).then_inc(x_evac, 1)

            def gate_copies(R, first, last, order, Pb):
                for n in range(first, last):
                    act.wait_ge(bc_done, R + n + 1)
                    if n == first > 0:
                        act.wait_ge(pair_done, Pb)
                    nc.scalar.activation(gate_b[:, order[n], :], gps[1 - n % 2][:, :], ACT.Copy).then_inc(gb_rdy, 1)

            def gate_slot(j, Q, R, rows_, order, Pb):
                if j == 0:
                    act.wait_ge(logit_done, Q + 1)
                    if not isinstance(Q, int) or Q:
                        act.wait_ge(lt_done, Q)
                    nc.scalar.activation(logit_t[0:rows_, :], gps[0][0:rows_, :], ACT.Copy).then_inc(logit_evac, 1)
                n = min(4, len(order)) - (len(order) == 4)
                if j == 1:
                    act.wait_ge(shift_rdy, Q + 1)
                    nc.scalar.activation(lg[:, :, 0:rows_ // 2], lg[:, :, 0:rows_ // 2], ACT.Exp).then_inc(exp_rdy, 1)
                if j == 2:
                    act.wait_ge(gt_done, Q + 1)
                    if not isinstance(R, int) or R:
                        act.wait_ge(bc_done, R)
                    nc.scalar.activation(gate_t, gps[0][0:12, :], ACT.Copy).then_inc(gt_evac, 1)
                    if not isinstance(Pb, int) or Pb > 8:
                        act.wait_ge(pair_done, Pb - 4)
                    gate_copies(R, 0, n, order, Pb)
                if j == 3:
                    gate_copies(R, n, len(order), order, Pb)

            def step(U, V, off, dest, bias, gates=None, x=None):
                for j in range(1, STEP - 1):
                    if j == 1 and gates:
                        gate_slot(0, *gates)
                    act.wait_ge(unit_done, U + j)
                    split_hi((j + 1) % 2, (off + j + 1) % RAW, V + (off + j + 1) // RAW)
                    dest_wait(dest, j - 1)
                    evacuate(main[(j - 1) % 2][:, :], dest(j - 1), bias(j - 1))
                    if x is not None:
                        rows_out(x, NBT + j - 1)
                    if gates:
                        gate_slot(j, *gates)

            def dest_wait(dest, u):
                if u in dest.waits:
                    for s_, v in dest.waits[u]:
                        act.wait_ge(s_, v)

            def shared_dest(waits):
                def dest(u):
                    return eo_sh[:, u, :]
                dest.waits = waits
                return dest

            def task_dest(t, S, Pb):
                def dest(u):
                    if u < KT:
                        return slots[:, bass.ds(t * KT + u, 1), :]
                    return eo_b[:, bass.ds(u % 4, 1), :]
                dest.waits = {
                    0: [(act_lo_rdy, (S + 1) * KT)],
                    KT: [(pair_done, Pb)],
                    KT + 4: [(pair_done, Pb + 5)],
                    KT + 6: [(pair_done, Pb + 6)],
                }
                return dest

            def biases(tile, first):
                return lambda u: tile[:, bass.ds(first + u, 1)]

            def change(U, V, off, dest, bias, S, chunk, shared=None):
                act.wait_ge(unit_done, U - 1)
                split_hi(0, off % RAW, V)
                dest_wait(dest, STEP - 2)
                evacuate(main[0][:, :], dest(STEP - 2), bias(STEP - 2))
                if shared:
                    for p in range(3):
                        act.wait_ge(sh_done, shared + p)
                        hand_over(S, chunk, (2 * p, 2 * p + 1), U)
                else:
                    hand_over(S, chunk, range(KT), U)
                act.wait_ge(unit_done, U)
                dest_wait(dest, STEP - 1)
                evacuate(main[1][:, :], dest(STEP - 1), bias(STEP - 1))
                if shared:
                    act.wait_ge(sh_done, shared + 3)
                    hand_over(S, chunk, (6, 7), U)
                split_hi(1, (off + 1) % RAW, V + (off + 1) // RAW)

            def first_step_out(h, U, dest, bias, x, S):
                V, off = U // RAW, U % RAW
                act.wait_ge(unit_done, U - 1)
                split_hi(0, off, V)
                evacuate(main[0][:, :], dest(STEP - 2), bias(STEP - 2))
                rows_out(x, NBT + STEP - 2)
                if h == 0:
                    hand_over(S, 0, range(KT), U)
                else:
                    first_outputs(h - 1, S - 1, top)
                act.wait_ge(unit_done, U)
                split_hi(1, off + 1, V)
                evacuate(main[1][:, :], dest(STEP - 1), bias(STEP - 1))
                rows_out(x, NBT + STEP - 1)
                if h == 0:
                    return
                V, off = (U + 2) // RAW, (U + 2) % RAW
                act.wait_ge(unit_done, U + 1)
                split_hi(0, off, V)
                second_outputs(h - 1, U, top)
                split_hi(1, off + 1, V)
                for k in range(KT):
                    nc.scalar.activation(act_hi[:, k, :], slots[:, k, :], ACT.Copy).then_inc(act_hi_rdy, 1)
                result(h - 1, top)

            def first_sums(h):
                act.wait_ge(pair_done, (h + 1) * PAIRS)
                for m in range(MT1):
                    act.wait_ge(unit_done, places(h + 1)[0] + (2 if h else 0) - MT1 + m + 1)
                    nc.scalar.activation(gate_b[:, m, :], top[m][:, :], ACT.Relu, bias=bias_t1[:, m:m + 1])\
                        .then_inc(h1_rdy, 1)

            def first_outputs(h, S, banks):
                for k in range(MT1):
                    act.wait_ge(h1_rdy, h * MT1 + k + 1)
                    act.wait_ge(act_free, (S - 1) * (KT - 1) + k + 1)
                    nc.scalar.activation(act_hi[:, k, :], gate_b[:, k, :], ACT.Copy).then_inc(act_hi_rdy, 2)

            def second_outputs(h, U, banks):
                for m in range(MT2):
                    if m == 0:
                        act.wait_ge(t2_done, h + 1)
                    else:
                        act.wait_ge(unit_done, U + 2)
                    nc.scalar.activation(eo_b[:, m, :], banks[m][:, :], ACT.Relu, bias=bias_t2[:, m:m + 1])\
                        .then_inc(h2_rdy, 1)

            def result(h, banks):
                act.wait_ge(y_done, h + 1)
                act.wait_ge(lt_done, (h + 1) * GATED + (h + 1 < HALVES))
                nc.scalar.activation(logit_t[0:1, :], banks[2][0:1, :], ACT.Copy).then_inc(y_rdy, 1)
                act.wait_ge(y_rdy, h + 1)
                act.dma_start(out[h:h + 1, :], logit_t[0:1, :]).then_inc(y_out, 16)
                act.wait_ge(y_out, 16 * (h + 1))

            def tower_slots(U, V, off, S, chunk, h_next=None, last=False):
                for j in (1, 2):
                    act.wait_ge(unit_done, U + j)
                    split_hi((j + 1) % 2, (off + j + 1) % RAW, V + (off + j + 1) // RAW)
                    if h_next is not None and j == 2:
                        rows_out(h_next, 0)
                        rows_out(h_next, 1)
                if last:
                    act.wait_ge(unit_done, U + 3)
                    split_hi(0, off, V + 1)
                    return
                act.wait_ge(unit_done, U + 3)
                split_hi(0, off, V + 1)
                if h_next is not None:
                    rows_out(h_next, 2)
                    rows_out(h_next, 3)
                    act.wait_ge(x_evac, h_next * XBANKS + 2 * NBT)
                hand_over(S, chunk, range(KT), U + 4)
                act.wait_ge(unit_done, U + 4)
                split_hi(1, (off + 1) % RAW, V + 1 + (off + 1) // RAW)

            for dst, src in ((bias0, b0), (bias1, b1), (bias_t1, b_top1), (bias_t2, b_top2), (w3, w_top3)):
                act.dma_start(dst[:, :], src).then_inc(consts_in, 16)
            act.dma_start(comb_sh[0:ONES_ROW, :], comb_s).then_inc(consts_in, 16)
            act.dma_start(comb_sh[ONES_ROW:ONES_ROW + 1, :], gs_b).then_inc(consts_in, 16)
            act.dma_start(comb_tk[0:ONES_ROW, :], comb_t).then_inc(consts_in, 16)
            act.wait_ge(chain, 4)
            nc.scalar.activation(warm[:, 1:2], warm[:, 0:1], ACT.Exp)
            split_hi(0, 0, 0)
            split_hi(1, 1, 0)
            for g in range(NBT):
                rows_out(0, g)
            act.wait_ge(x_evac, 2 * NBT)
            hand_over(0, 4 * KT, range(KT), 0)
            act.wait_ge(pre_rdy, 1)
            act.wait_ge(consts_in, 16 * 8)
            for h in range(HALVES):
                (first, u0), (sf, s0), q0, r0, p0 = places(h), steps(h), h * GATED, h * BCASTS, h * PAIRS
                v0 = u0 // RAW
                dest, bias = shared_dest({0: [(pair_done, p0)]} if h else {}), biases(bias0, 0)
                step(first, first // RAW, first % RAW, dest, bias, (q0, r0, 2 * NE, [4, 5], p0), x=h)
                first_step_out(h, first + STEP, dest, bias, h, s0 + 1)

                def task0(t, shared=None):
                    U, V = u0 + U_T0 + t * STEP, (u0 + U_T0) // RAW + t * (STEP // RAW)
                    S, Pb = s0 + 1 + t, p0 + 8 + t * 8
                    dest, bias = task_dest(t, S, Pb), biases(bias0, STEP + t * STEP)
                    step(U, V, 0, dest, bias, (q0 + 1 + t, r0 + 2 + t * 6, 2 * NG, [4, 0, 2, 3, 5, 1], Pb))
                    change(U + STEP, V + STEP // RAW, 0, dest, bias, S + 1, (t + 1) * KT, shared=shared)

                with act.Fori(0, T - 1) as t:
                    task0(t)
                task0(T - 1, shared=h * 4 * T + 1 + (T - 1) * 4)
                U, S = u0 + U_SH1, s0 + T + 1
                V = U // RAW
                dest, bias = shared_dest({0: [(pair_done, p0 + 8 * T + 4)]}), biases(bias1, 0)
                step(U, V, 0, dest, bias)
                D0 = u0 + U_DENSE
                act.wait_ge(unit_done, D0 - 1)
                act.wait_ge(dctx_in[0], 16 * (h + 1))
                split_hi(0, 0, D0 // RAW, parts=DENSE, cols=DENSE_COLS)
                evacuate(main[0][:, :], dest(STEP - 2), bias(STEP - 2))
                hand_over(S + 1, 0, range(KT), D0)
                act.wait_ge(unit_done, D0)
                act.wait_ge(dctx_in[1], 16 * (h + 1))
                split_hi(1, 1, D0 // RAW, parts=DENSE, cols=DENSE_COLS)
                U, V, off = u0 + U_T1, (u0 + U_T1) // RAW, U_T1 % RAW
                act.wait_ge(unit_done, U - 1)
                split_hi(0, off, V)
                evacuate(main[1][:, :], dest(STEP - 1), bias(STEP - 1))
                act.wait_ge(unit_done, U)
                split_hi(1, off + 1, V)
                own = [0, 2, 3, 1]
                S, Pb, Q, R = S + 1, p0 + 8 * (T + 1), q0 + T + 1, r0 + 2 + 6 * T
                dest, bias = task_dest(0, S, Pb), biases(bias1, STEP)
                step(U, V, off, dest, bias, (Q, R, 2 * NG, own, Pb))
                change(U + STEP, V + STEP // RAW, off, dest, bias, S + 1, KT)
                Un, Vn = u0 + U_T1N, V + STEP // RAW
                both = STEP + MT1

                def task1(n, last=False):
                    t, Sn, Pn, Ut, Vt = n + 1, S + 1 + n * 2, Pb + 8 + n * 8, Un + n * both, Vn + n * (both // RAW)
                    dest, bias = task_dest(t, Sn, Pn), biases(bias1, STEP + t * STEP)
                    step(Ut, Vt, off, dest, bias, (Q + 1 + n, R + 4 + n * 4, 2 * NG, own, Pn))
                    change(Ut + STEP, Vt + STEP // RAW, off, dest, bias, Sn + 1, (t - 1) * KT)
                    if last:
                        act.wait_ge(pair_done, Pn + 8)
                    tower_slots(Ut + STEP, Vt + STEP // RAW, off, Sn + 2, (t if last else t + 1) * KT)

                with act.Fori(0, T - 2) as n:
                    task1(n)
                task1(T - 2, last=True)
                U = Un + (T - 1) * both
                if h + 1 < HALVES:
                    tower_slots(U, U // RAW, off, steps(h + 1)[0], 4 * KT, h_next=h + 1)
                    first_sums(h)
            tower_slots(U, U // RAW, off, None, None, last=True)
            first_sums(HALVES - 1)
            S, U = s0 + HALF_STEPS, U + MT1
            first_outputs(HALVES - 1, S, main + gps)
            act.wait_ge(unit_done, U)
            split_hi(1, (off + 1) % RAW, U // RAW + (off + 1) // RAW)
            second_outputs(HALVES - 1, U, main + gps)
            result(HALVES - 1, main + gps)

        @block.vector
        def _(dve):
            class Count:
                start, n = 0, 0

            links = Count()

            def link(ins):
                links.n += 1
                ins.then_inc(chain, 1)
                return links.start + links.n

            def after(value):
                dve.wait_ge(chain, value)

            def split_lo(U, slot, rawslot, turn, parts=P, cols=KT * P):
                dve.wait_ge(raw_in[rawslot], turn * 16 + 16)
                dve.wait_ge(hi_split, U + 1)
                nc.vector.tensor_tensor(w_lo[0:parts, slot, 0:cols], raw[0:parts, rawslot, 0:cols],
                                        w_hi[0:parts, slot, 0:cols], ALU.subtract).then_inc(lo_split, 1)

            def hand_over(S, chunk, ks):
                for k in ks:
                    dve.wait_ge(act_hi_rdy, S * KT + k + 1)
                    nc.vector.tensor_tensor(act_lo[:, bass.ds(k, 1), :], slots[:, bass.ds(chunk + k, 1), :],
                                            act_hi[:, bass.ds(k, 1), :], ALU.subtract).then_inc(act_lo_rdy, 1)

            def split_gates(q_in, Q, n, R):
                dve.wait_ge(gw_in, q_in)
                if not isinstance(Q, int) or Q:
                    dve.wait_ge(logit_done, Q)
                    dve.wait_ge(gb_rdy, R)
                src = gw_raw[:, 0:KT * n].rearrange("p (k n) -> p k n", k=KT)
                nc.vector.tensor_copy(gw[:, :, 0:n], src).then_inc(gw_step, 1)
                dve.wait_ge(gw_step, Q + 1)
                nc.vector.tensor_tensor(gw[:, :, n:2 * n], src, gw[:, :, 0:n], ALU.subtract).then_inc(gw_rdy, 1)

            def softmax(Q, n, shared_at=None):
                t = slice(0, n)
                dve.wait_ge(lt_done, Q + 1)
                ps = gps[1][:, 0:NBT * n].rearrange("p (b n) -> p b n", b=NBT)
                after(link(nc.vector.tensor_reduce(mx[:, :], ps, AX.X, ALU.max)))
                nc.vector.tensor_tensor(lg[:, :, t], ps, mx[:, :, None].broadcast_to([P, NBT, n]),
                                        ALU.subtract).then_inc(shift_rdy, 1)
                dve.wait_ge(exp_rdy, Q + 1)
                after(link(nc.vector.tensor_reduce(mx[:, :], lg[:, :, t], AX.X, ALU.add)))
                after(link(nc.vector.reciprocal(rs[:, :], mx[:, :])))
                inv = rs[:, :, None].broadcast_to([P, NBT, n])
                if n == NE:
                    after(link(nc.vector.tensor_tensor(gsh[:, :, :], lg[:, :, t], inv, ALU.mult)))
                    last = link(nc.vector.tensor_copy(g6[:, :, 4:6], gsh[:, :, NE - 2:NE]))
                else:
                    last = link(nc.vector.tensor_tensor(g6[:, :, 0:n], lg[:, :, t], inv, ALU.mult))
                    if shared_at is not None:
                        last = link(nc.vector.tensor_copy(g6[:, :, 4:6], gsh[:, :, bass.ds(shared_at, 2)]))
                after(last)
                after(link(nc.vector.tensor_copy(g12[:, :, 0:6], g6[:, :, :])))
                nc.vector.tensor_tensor(g12[:, :, 6:12], g6[:, :, :], g12[:, :, 0:6], ALU.subtract)\
                    .then_inc(g12_rdy, 1)

            def gate(j):
                return gate_b[:, j:j + 1, :].broadcast_to([P, 2, N])

            def gating(kind, t, E, R, Pb, shb=None):
                tmp = prod[:, :, :]
                order = {"shared": [4, 5], "layer0": [4, 0, 2, 3, 5, 1], "layer1": [0, 2, 3, 1]}[kind]
                seen = {}

                def pair(first, p):
                    return slots[:, bass.ds(first * KT + 2 * p, 2), :]

                def sh(x, p):
                    return eo_sh[:, x * KT + 2 * p:x * KT + 2 * p + 2, :]

                def out_of_psum(u):
                    dve.wait_ge(evac_done, E + u + 2)

                def mul(dst, src, j, name, needs):
                    dve.wait_ge(gb_rdy, R + order.index(j) + 1)
                    for n in needs:
                        wait(n)
                    seen[name] = (chain, link(nc.vector.tensor_tensor(dst, src, gate(j), ALU.mult)))

                def add(dst, x, needs, name, signal=None):
                    for n in needs:
                        wait(n)
                    ins = nc.vector.tensor_tensor(dst, dst, x, ALU.add)
                    if signal is None:
                        signal = (chain, link(ins))
                    else:
                        ins.then_inc(signal[0], 1)
                    seen[name] = signal

                def wait(name):
                    if name in seen:
                        dve.wait_ge(*seen[name])

                if not isinstance(Pb, int) or Pb:
                    seen["tmp read"] = (pair_done, Pb)

                def a_ops(p):
                    done = (pair_done, Pb + p + 1)
                    if kind == "shared":
                        def first():
                            out_of_psum(2 * p)
                            dve.wait_ge(gb_rdy, R + 1)
                            nc.vector.tensor_tensor(pair(4, p), sh(0, p), gate(4), ALU.mult).then_inc(pair_done, 1)
                        return [first]
                    a = pair(t, p)
                    if kind == "layer1":
                        return [
                            lambda: (out_of_psum(2 * p), mul(a, a, 0, "own", [])),
                            lambda: mul(tmp, sh(0, p), 2, "s8", ["tmp read"]),
                            lambda: add(a, tmp, ["s8"], "tmp read"),
                            lambda: mul(tmp, sh(1, p), 3, "s9", ["tmp read"]),
                            lambda: add(a, tmp, ["s9"], "tmp read", done),
                        ]
                    return [
                        lambda: (out_of_psum(2 * p), mul(tmp, a, 4, "sh", ["tmp read"])),
                        lambda: add(pair(4, p), tmp, ["sh"], "tmp read"),
                        lambda: mul(a, a, 0, "own", ["sh"]),
                        lambda: mul(tmp, sh(0, p), 2, "s8", ["tmp read"]),
                        lambda: add(a, tmp, ["s8"], "tmp read"),
                        lambda: mul(tmp, sh(1, p), 3, "s9", ["tmp read"]),
                        lambda: add(a, tmp, ["s9"], "tmp read", done),
                    ]

                def b_ops(p):
                    done = (pair_done, Pb + 5 + p)

                    def gated_first(then):
                        dve.wait_ge(pair_done, Pb + p + 1)
                        then()

                    if kind == "shared":
                        return [lambda: (out_of_psum(KT + 2 * p), mul(tmp, sh(1, p), 5, "sh", ["tmp read"])),
                                lambda: gated_first(lambda: add(pair(4, p), tmp, ["sh"], "tmp read", done))]
                    b = eo_b[:, 2 * (p % 2):2 * (p % 2) + 2, :]
                    own = lambda: gated_first(lambda: add(pair(t, p), b, ["own"], "own done", done))
                    if kind == "layer1":
                        return [lambda: (out_of_psum(KT + 2 * p), mul(b, b, 1, "own", [])), own]
                    return [lambda: (out_of_psum(KT + 2 * p), mul(tmp, b, 5, "sh", ["tmp read"])),
                            lambda: add(pair(4, p), tmp, ["sh"], "tmp read", (sh_done, shb + p + 1)),
                            lambda: mul(b, b, 1, "own", ["sh"]), own]

                return a_ops, b_ops

            def run(ops):
                for op in ops:
                    op()

            def step(U, V, off, ops=None, gates=None, split=None, plan=None):
                queue = []
                if plan:
                    for p in range(4):
                        queue += ops[0](p)
                    for p in range(3):
                        queue += ops[1](p)
                for j in range(1, STEP - 1):
                    split_lo(U + j + 1, (j + 1) % 2, (off + j + 1) % RAW, V + (off + j + 1) // RAW)
                    if j == 1 and gates:
                        softmax(*gates)
                    if j == 8 and split:
                        split_gates(*split)
                    if plan and j >= 3:
                        done = sum(plan[:j - 3])
                        run(queue[done:done + plan[j - 3]])
                    elif ops and j >= 3:
                        p, second = (j - 3) // 2, (j - 3) % 2
                        now = ops[0](p) if p < 4 else ops[1](p - 4)
                        cut = (len(now) + 1) // 2
                        run(now[cut:] if second else now[:cut])

            def change(U, V, off, S, chunk, ops, shared=False):
                split_lo(U, 0, off, V)
                b2, b3 = ops[1](2), ops[1](3)
                if shared:
                    hand_over(S, chunk, range(0, 6))
                    run(b3[:2])
                    hand_over(S, chunk, (6, 7))
                    split_lo(U + 1, 1, off + 1, V)
                    run(b2[2:] + b3[2:])
                else:
                    hand_over(S, chunk, range(KT))
                    split_lo(U + 1, 1, off + 1, V)
                    run(b2 + b3)

            def tower_slots(U, V, off, S, chunk, last=False):
                for j in (1, 2):
                    split_lo(U + j + 1, (j + 1) % 2, (off + j + 1) % RAW, V + (off + j + 1) // RAW)
                split_lo(U + 4, 0, off, V + 1)
                if not last:
                    hand_over(S, chunk, range(KT))
                    split_lo(U + 5, 1, (off + 1) % RAW, V + 1 + (off + 1) // RAW)

            def first_outputs(S):
                for k in range(MT1):
                    dve.wait_ge(act_hi_rdy, S * KT + 2 * (k + 1))
                    nc.vector.tensor_tensor(act_lo[:, k, :], gate_b[:, k, :], act_hi[:, k, :], ALU.subtract)\
                        .then_inc(act_lo_rdy, 2)

            def loop_links(i, per):
                begun = links.start + links.n
                links.start, links.n = begun + i * per, 0
                return begun

            def end_links(begun, turns, per):
                assert links.n == per, (links.n, per)
                links.start, links.n = begun + turns * per, 0

            nc.vector.memset(gw[:, :, :].bitcast(f32), 0.0).then_inc(chain, 1)
            nc.vector.memset(logit_t[:, :], 1.0).then_inc(chain, 1)
            nc.vector.memset(g6[:, :, :], 0.0).then_inc(chain, 1)
            nc.vector.memset(warm[:, :], 0.0).then_inc(chain, 1)
            nc.vector.memset(g12[:, :, :].bitcast(f32), 0.0).then_inc(chain, 1)
            links.n = 5
            after(5)
            dve.wait_ge(ident_rdy, 16)
            after(link(nc.vector.tensor_tensor(pick[:, :], ident[0:12, 0:6], ident[0:12, 6:12], ALU.add)))
            nc.vector.tensor_copy(ident_r[:, :], ident[:, :]).then_inc(pre_rdy, 1)
            split_gates(16, 0, NE, 0)
            split_lo(0, 0, 0, 0)
            split_lo(1, 1, 1, 0)
            hand_over(0, 4 * KT, range(KT))
            plan0 = [3] * 12
            plan0_last = [3] * 10 + [4, 4]
            for h in range(HALVES):
                (first, u0), (sf, s0), e0, q0, r0, p0 = \
                    places(h), steps(h), h * EUNITS, h * GATED, h * BCASTS, h * PAIRS
                gin = h * GATE_LOADS + 16
                ops = gating("shared", 4, e0, r0, p0)
                step(first, first // RAW, first % RAW, ops, (q0, NE), (gin + 32, q0 + 1, NG, r0 + 2))
                U = first + STEP
                if h == 0:
                    change(U, U // RAW, U % RAW, s0 + 1, 0, ops)
                else:
                    split_lo(U, 0, U % RAW, U // RAW)
                    first_outputs(s0)
                    split_lo(U + 1, 1, (U + 1) % RAW, U // RAW)
                    run(ops[1](2))
                    change(U + 2, (U + 2) // RAW, 0, s0 + 1, 0, (None, lambda p: ops[1](3) if p == 3 else []))

                def task0(t, plan, last=False):
                    U, V = u0 + U_T0 + t * STEP, (u0 + U_T0) // RAW + t * (STEP // RAW)
                    ops = gating("layer0", t, e0 + STEP + t * STEP, r0 + 2 + t * 6, p0 + 8 + t * 8,
                                 h * 4 * T + t * 4)
                    step(U, V, 0, ops, (q0 + 1 + t, NG, t * 2), (gin + 64 + t * 32, q0 + 2 + t, NG, r0 + 8 + t * 6),
                         plan)
                    change(U + STEP, V + STEP // RAW, 0, s0 + 2 + t, (t + 1) * KT, ops, shared=last)

                with dve.Fori(0, T - 1) as t:
                    begun = loop_links(t, LINKS_L0)
                    task0(t, plan0)
                end_links(begun, T - 1, LINKS_L0)
                task0(T - 1, plan0_last, last=True)
                U = u0 + U_SH1
                step(U, U // RAW, 0)
                D0, U, off = u0 + U_DENSE, u0 + U_T1, U_T1 % RAW
                V, S = U // RAW, s0 + T + 2
                dve.wait_ge(dctx_in[0], 16 * (h + 1))
                split_lo(D0, 0, 0, D0 // RAW, parts=DENSE, cols=DENSE_COLS)
                hand_over(S, 0, range(KT))
                dve.wait_ge(dctx_in[1], 16 * (h + 1))
                split_lo(D0 + 1, 1, 1, D0 // RAW, parts=DENSE, cols=DENSE_COLS)
                split_lo(U, 0, off, V)
                split_lo(U + 1, 1, off + 1, V)
                E, R, Pb, Q = e0 + (T + 2) * STEP, r0 + 2 + 6 * T, p0 + 8 * (T + 1), q0 + T + 1
                gin = gin + 32 * (T + 2)
                ops = gating("layer1", 0, E, R, Pb)
                step(U, V, off, ops, (Q, NG), (gin, Q + 1, NG, R + 4))
                change(U + STEP, V + STEP // RAW, off, S + 1, KT, ops)
                Un, Vn, both = U + STEP, V + STEP // RAW, STEP + MT1

                def task1(n, split, last=False):
                    t, Sn, Ut, Vt = n + 1, S + 1 + n * 2, Un + n * both, Vn + n * (both // RAW)
                    ops = gating("layer1", t, E + STEP + n * STEP, R + 4 + n * 4, Pb + 8 + n * 8)
                    step(Ut, Vt, off, ops, (Q + 1 + n, NG), split)
                    change(Ut + STEP, Vt + STEP // RAW, off, Sn + 1, (t - 1) * KT, ops)
                    tower_slots(Ut + STEP, Vt + STEP // RAW, off, Sn + 2, (t if last else t + 1) * KT)

                with dve.Fori(0, T - 2) as n:
                    begun = loop_links(n, LINKS_L1)
                    task1(n, (gin + 32 + n * 32, Q + 2 + n, NG, R + 8 + n * 4))
                end_links(begun, T - 2, LINKS_L1)
                more = h + 1 < HALVES
                task1(T - 2, ((h + 1) * GATE_LOADS + 16, (h + 1) * GATED, NE, (h + 1) * BCASTS) if more else None,
                      last=True)
                U = Un + (T - 1) * both
                if more:
                    tower_slots(U, U // RAW, off, steps(h + 1)[0], 4 * KT)
            tower_slots(U, U // RAW, off, None, None, last=True)
            first_outputs(s0 + HALF_STEPS)
            U += MT1
            split_lo(U + 1, 1, (off + 1) % RAW, (U + 1) // RAW)


LINKS_L0 = 6 + 4 * 6 + 4 * 2
LINKS_L1 = 5 + 4 * 4 + 4 * 1


def _units(w, strips):
    e, k, _ = w.shape
    return np.ascontiguousarray(
        w.reshape(e, k // P, P, strips, P).transpose(0, 3, 2, 1, 4).reshape(e * strips, P, k))


def kernel(dense_ctx, ids, tbl_0, tbl_1, tbl_2, tbl_3, tbl_4, W_top1, b_top1, W_top2, b_top2, W_top3,
           L0_rec_W0, L0_rec_b0, L0_rec_G0w, L0_rec_G0b, L0_rec_Gs0w, L0_rec_Gs0b, L0_rec_W1, L0_rec_b1,
           L0_rec_G1w, L0_rec_G1b):
    import concourse.bacc as bacc
    from concourse.bass_utils import run_bass_kernel_spmd as run

    a = {k: np.asarray(v) for k, v in locals().items() if k not in ("bacc", "run")}
    order = list(EXPERTS)

    def kt_cols(w):
        k, n = w.shape
        return np.ascontiguousarray(w.reshape(k // P, P, n).transpose(1, 0, 2).reshape(P, -1))

    def per_part(v):
        return np.ascontiguousarray(v.reshape(-1, P).T)

    def combine(n):
        c = np.zeros((ONES_ROW, n), np.float32)
        c[np.arange(2 * n), np.arange(2 * n) % n] = 1.0
        return c

    w_top1 = a["W_top1"]
    laid = {
        "ids": np.ascontiguousarray(a["ids"].T.reshape(5 * HALVES * NBT, P).T),
        "dense_t": np.ascontiguousarray(a["dense_ctx"].T),
        "tbl_0": a["tbl_0"], "tbl_1": a["tbl_1"], "tbl_2": a["tbl_2"], "tbl_3": a["tbl_3"], "tbl_4": a["tbl_4"],
        "w0": _units(a["L0_rec_W0"][order], KT),
        "w1": _units(a["L0_rec_W1"][order], KT),
        "w_top": _units(w_top1[:T * D].reshape(T, D, TOP1), MT1),
        "w_dense": np.ascontiguousarray(w_top1[T * D:].reshape(DENSE, 2, TOP1 // 2).transpose(1, 0, 2)),
        "w_top2": np.ascontiguousarray(
            a["W_top2"].reshape(2, 2, P, TOP2).transpose(0, 2, 1, 3).reshape(2, P, 2 * TOP2)),
        "w_top3": per_part(a["W_top3"]),
        "b0": per_part(a["L0_rec_b0"][order]), "b1": per_part(a["L0_rec_b1"][order]),
        "b_top1": per_part(a["b_top1"]), "b_top2": per_part(a["b_top2"]),
        "gs_w": kt_cols(a["L0_rec_Gs0w"]),
        "g_w": np.stack([kt_cols(w) for w in (*a["L0_rec_G0w"], *a["L0_rec_G1w"])]),
        "g_b": np.concatenate([a["L0_rec_G0b"], a["L0_rec_G1b"]]),
        "comb_s": combine(NE), "comb_t": combine(NG),
        "gs_b": a["L0_rec_Gs0b"].reshape(1, NE),
        "ident_in": np.eye(P, dtype=np.float32),
    }
    nc = bacc.Bacc("TRN2", target_bir_lowering=False, num_devices=1)
    args = {n: nc.dram_tensor(f"in_{n}", v.shape, mybir.dt.from_np(v.dtype), kind="ExternalInput").ap()
            for n, v in laid.items()}
    y = nc.dram_tensor("y", (HALVES, N), mybir.dt.float32, kind="ExternalOutput").ap()
    build(nc, out=y, **args)
    r = run(nc, [{f"in_{n}": v for n, v in laid.items()}], core_ids=[0])
    return np.asarray(r.results[0]["y"]).reshape(B, 1)
```

```python
from contextlib import ExitStack

import numpy as np
import concourse.bass as bass
from concourse import mybir

B, D, T, NE = 1024, 1024, 4, 10
P = 128
HALVES, N = 2, 512
KT = D // P
NBT = N // P
EXPERTS = (8, 9, 0, 1, 2, 3, 4, 5, 6, 7)
DENSE = 16
TOP1, TOP2 = 512, 256
MT1, MT2 = TOP1 // P, TOP2 // P
STEP = 2 * KT
NG = T
LOGIT_ROWS = 66
ONES_ROW = 32

U_SH0, U_T0, U_SH1, U_DENSE = 0, STEP, STEP * (T + 1), STEP * (T + 2)
U_T1 = U_DENSE + 2
U_T1N = U_T1 + STEP
HALF_UNITS = U_T1N + (T - 1) * (STEP + MT1) + MT1
EUNITS = 2 * STEP * (T + 1)
HALF_STEPS = 2 * (T + 1) + T
GATED = 2 * T + 1
PAIRS = 8 * (T + 1) + 8 * T
BCASTS = 2 + 6 * T + 4 * T
GATE_LOADS = 16 + 32 * 2 * T
DENSE_COLS = TOP1 // 2 + N
Q4 = 4
ROWSETS = 5 * NBT
IDX = NBT + (ROWSETS * HALVES - NBT) * Q4
RAW = 4


def build(nc, ids, dense_t, tbl_0, tbl_1, tbl_2, tbl_3, tbl_4, w0, w1, w_top, w_dense, w_top2, w_top3,
          b0, b1, b_top1, b_top2, gs_w, g_w, g_b, comb_s, comb_t, gs_b, ident_in, out):
    f32, f32r, i32 = mybir.dt.float32, mybir.dt.float32r, mybir.dt.int32
    ALU, ACT, AX = mybir.AluOpType, mybir.ActivationFunctionType, mybir.AxisListType
    tables = (tbl_0, tbl_1, tbl_2, tbl_3, tbl_4)

    ctx = ExitStack()
    with ctx:
        def sb(name, shape, dt=f32):
            return ctx.enter_context(nc.sbuf_tensor(name, shape, dt))

        def bank(name):
            return ctx.enter_context(nc.psum_tensor(name, [P, N], f32))

        def sem(name):
            return ctx.enter_context(nc.semaphore(name))

        slots = sb("slots", [P, 5 * KT, N])
        act_hi = sb("act_hi", [P, KT, N], f32r)
        act_lo = sb("act_lo", [P, KT, N], f32r)
        eo_sh = sb("eo_sh", [P, 2 * KT, N])
        eo_b = sb("eo_b", [P, 4, N])
        raw = sb("raw", [P, RAW, KT * P])
        w_hi = sb("w_hi", [P, 2, KT * P], f32r)
        w_lo = sb("w_lo", [P, 2, KT * P], f32r)
        gate_b = sb("gate_b", [P, 6, N])
        prod = sb("prod", [P, 2, N])
        gw_raw = sb("gw_raw", [P, KT * NE])
        gw = sb("gw", [P, KT, LOGIT_ROWS], f32r)
        logit_t = sb("logit_t", [ONES_ROW + 1, N])
        gate_t = gw[0:12, :, :].rearrange("p k n -> p (k n)")[:, 0:N]
        comb = sb("comb", [ONES_ROW + 1, NE + NG])
        comb_sh, comb_tk = comb[:, 0:NE], comb[:, NE:]
        lg = sb("lg", [P, NBT, NE])
        small = sb("small", [P, 2 * NBT + 2])
        mx, rs, warm = small[:, 0:NBT], small[:, NBT:2 * NBT], small[:, 2 * NBT:]
        gsh = sb("gsh", [P, NBT, NE])
        g6 = sb("g6", [P, NBT, 6])
        g12 = sb("g12", [P, NBT, LOGIT_ROWS], f32r)
        pick = sb("pick", [12, 6], f32r)
        ident = prod[:, 0, 0:P]
        ident_r = sb("ident_r", [P, P], f32r)
        idx = sb("idx", [P, IDX], i32)
        bias0 = sb("bias0", [P, NE * KT])
        bias1 = sb("bias1", [P, NE * KT])
        tower_c = sb("tower_c", [P, MT1 + 2 * MT2])
        bias_t1, bias_t2, w3 = tower_c[:, 0:MT1], tower_c[:, MT1:MT1 + MT2], tower_c[:, MT1 + MT2:]

        main = [bank(f"main{i}") for i in range(2)]
        gps = [bank(f"gps{i}") for i in range(2)]
        top = [bank(f"top{i}") for i in range(MT1)]

        consts_in = sem("consts_in")
        idx_in = sem("idx_in")
        raw_in = [sem(f"raw_in{i}") for i in range(RAW)]
        dctx_in = [sem(f"dctx_in{i}") for i in range(2)]
        gw_in = sem("gw_in")
        ident_rdy = sem("ident_rdy")
        x_in = [sem(f"x_in{i}") for i in range(2)]
        idx_rdy = sem("idx_rdy")
        x0_in = [sem(f"x0_in{i}") for i in range(NBT)]
        x0_even = sem("x0_even")
        x0_odd = sem("x0_odd")
        x0_turned = sem("x0_turned")
        y_out = sem("y_out")
        hi_split = sem("hi_split")
        lo_split = sem("lo_split")
        act_hi_rdy = sem("act_hi_rdy")
        act_lo_rdy = sem("act_lo_rdy")
        act_free = sem("act_free")
        unit_done = sem("unit_done")
        evac_done = sem("evac_done")
        x_done = sem("x_done")
        pair_done = sem("pair_done")
        sh_done = sem("sh_done")
        gw_rdy = sem("gw_rdy")
        gw_step = sem("gw_step")
        logit_done = sem("logit_done")
        logit_evac = sem("logit_evac")
        lt_done = sem("lt_done")
        shift_rdy = sem("shift_rdy")
        exp_rdy = sem("exp_rdy")
        g12_rdy = sem("g12_rdy")
        gt_done = sem("gt_done")
        gt_evac = sem("gt_evac")
        bc_done = sem("bc_done")
        gb_rdy = sem("gb_rdy")
        chain = sem("chain")
        h1_rdy = sem("h1_rdy")
        t2_done = sem("t2_done")
        h2_rdy = sem("h2_rdy")
        y_done = sem("y_done")
        y_rdy = sem("y_rdy")
        pre_rdy = sem("pre_rdy")

        block = ctx.enter_context(nc.Block())

        def rows(g):
            return (4, g) if g < NBT else (g // NBT - 1, g % NBT)

        def stage(g):
            return eo_b[:, 2 * (g % 2):2 * (g % 2) + 2, :].rearrange("p a (s n) -> p (a s) n", s=2)

        def set_no(h, g):
            return h * ROWSETS + g - NBT

        whole = [eo_sh[:, 2 * i:2 * i + 2, :].rearrange("p a n -> p (a n)") for i in range(NBT)]
        ordered = [eo_sh[:, KT + 2 * i:KT + 2 * i + 2, :].rearrange("p a n -> p (a n)") for i in range(NBT)]

        def by_order(i):
            return (ordered[i].rearrange("p (k q c) -> p k q c", k=KT, q=Q4),
                    whole[i].rearrange("p (q k c) -> p k q c", q=Q4, k=KT))

        x0_bank = [main[0], gps[0], main[1], gps[1]] + top

        def places(h):
            return h * HALF_UNITS, h * (HALF_UNITS + 2)

        def steps(h):
            return h * HALF_STEPS, h * (HALF_STEPS + 1)

        @block.sync
        def _(sp):
            def unit(src, i, slot, U, parts=P, cols=KT * P):
                if not isinstance(U, int) or U >= RAW:
                    sp.wait_ge(hi_split, U - RAW + 1)
                    sp.wait_ge(lo_split, U - RAW + 1)
                sp.dma_start(raw[0:parts, slot, 0:cols],
                             src[bass.ds(i, 1), 0:parts, :].rearrange("a p n -> p (a n)"))\
                    .then_inc(raw_in[slot], 16)

            def stream(src, first, count, U, off, start=0):
                with sp.Fori(start, count // RAW) as i:
                    for c in range(RAW):
                        unit(src, first + i * RAW + c, (off + c) % RAW, U + i * RAW + c)

            def gate_load(g, q):
                sp.wait_ge(gw_rdy, q)
                sp.wait_ge(lt_done, q)
                sp.dma_start(gw_raw[:, 0:KT * NG], g_w[bass.ds(g, 1), :, :].rearrange("a p n -> p (a n)"))\
                    .then_inc(gw_in, 16)
                sp.dma_start(comb_tk[ONES_ROW:ONES_ROW + 1, :], g_b[bass.ds(g, 1), :]).then_inc(gw_in, 16)

            def top2(h, U):
                for d in range(2):
                    unit(w_top2, d, (U + d) % RAW, U + d, cols=2 * TOP2)

            def gated_stream(src, first, U, off, g, q, start=0):
                stream(src, first, STEP // 2, U, off, start)
                gate_load(g, q)
                stream(src, first + STEP // 2, STEP // 2, U + STEP // 2, off)

            sp.dma_start(idx[:, :], ids).then_inc(idx_in, 16)
            sp.dma_start(ident, ident_in).then_inc(ident_rdy, 16)
            sp.dma_start(gw_raw[:, :], gs_w).then_inc(gw_in, 16)
            for h in range(HALVES):
                (first, base), gated = places(h), h * GATED
                if h == 0:
                    for c in range(RAW):
                        if c:
                            sp.wait_ge(x0_in[c], 16)
                        unit(w0, c, c, c)
                gated_stream(w0, 0, first, first % RAW, 0, gated + 1, start=1 if h == 0 else 0)
                if h:
                    top2(h - 1, first + STEP)
                with sp.Fori(0, T) as t:
                    gated_stream(w0, STEP + t * STEP, base + U_T0 + t * STEP, 0, t + 1, gated + 2 + t)
                stream(w1, 0, STEP, base + U_SH1, 0)
                for d in range(2):
                    slot = (U_DENSE + d) % RAW
                    unit(w_dense, d, slot, base + U_DENSE + d, parts=DENSE, cols=TOP1 // 2)
                    sp.dma_start(raw[0:DENSE, slot, TOP1 // 2:DENSE_COLS], dense_t[:, h * N:(h + 1) * N])\
                        .then_inc(dctx_in[d], 16)
                off = U_T1 % RAW
                gated_stream(w1, STEP, base + U_T1, off, T + 1, gated + T + 2)
                with sp.Fori(0, T - 2) as t:
                    gated_stream(w1, 2 * STEP + t * STEP, base + U_T1N + t * (STEP + MT1), off, T + 2 + t,
                                 gated + T + 3 + t)
                    stream(w_top, t * MT1, MT1, base + U_T1N + STEP + t * (STEP + MT1), off)
                late = base + U_T1N + (T - 2) * (STEP + MT1)
                stream(w1, STEP * T, STEP // 2, late, off)
                if h + 1 < HALVES:
                    sp.wait_ge(gw_rdy, gated + GATED)
                    sp.dma_start(gw_raw[:, :], gs_w).then_inc(gw_in, 16)
                stream(w1, STEP * T + STEP // 2, STEP // 2, late + STEP // 2, off)
                stream(w_top, (T - 2) * MT1, MT1, late + STEP, off)
                stream(w_top, (T - 1) * MT1, MT1, late + STEP + MT1, off)
            top2(HALVES - 1, late + STEP + 2 * MT1)

        @block.gpsimd
        def _(pool):
            pool.wait_ge(idx_in, 16)
            for bt in range(NBT):
                pool.indirect_dma_start(whole[bt], None, tbl_4, bass.IndirectOffsetOnAxis(ap=idx[:, bt:bt + 1], axis=0))\
                    .then_inc(x0_in[bt], 16)
            pool.wait_ge(x0_in[NBT - 1], 16)
            pool.wait_ge(idx_rdy, Q4)
            for h in range(HALVES):
                if h:
                    pool.wait_ge(pair_done, h * PAIRS)
                for g in range(0 if h else NBT, ROWSETS):
                    t, bt = rows(g)
                    if set_no(h, g) >= 2 and g >= 2:
                        pool.wait_ge(x_done, set_no(h, g) - 1)
                    for s in range(Q4):
                        c = NBT + ((t * HALVES + (h if t < T else 0)) * NBT + bt) * Q4 + s
                        pool.indirect_dma_start(
                            stage(g)[:, s, :], None, tables[t].rearrange("v (q n) -> (v q) n", q=Q4),
                            bass.IndirectOffsetOnAxis(ap=idx[:, c:c + 1], axis=0)).then_inc(x_in[g % 2], 16)

        @block.tensor
        def _(pe):
            def three(dst, lhs_hi, lhs_lo, rhs_hi, rhs_lo, start, stop):
                nc.tensor.matmul(dst, lhs_hi, rhs_hi, start=start, stop=False)
                nc.tensor.matmul(dst, lhs_hi, rhs_lo, start=False, stop=False)
                return nc.tensor.matmul(dst, lhs_lo, rhs_hi, start=False, stop=stop)

            def unit(dst, slot, U, S=None, last=False, start=True, stop=True, between=None):
                pe.wait_ge(hi_split, U + 1)
                pe.wait_ge(lo_split, U + 1)
                for k in range(KT):
                    if S is not None:
                        pe.wait_ge(act_hi_rdy, S * KT + k + 1)
                        pe.wait_ge(act_lo_rdy, S * KT + k + 1)
                    w = slice(k * P, (k + 1) * P)
                    mm = three(dst[:, :], w_hi[:, slot, w], w_lo[:, slot, w], act_hi[:, k, :], act_lo[:, k, :],
                               start and k == 0, stop and k == KT - 1)
                    if k == KT - 1:
                        mm.then_inc(unit_done, 1)
                    elif last:
                        mm.then_inc(act_free, 1)
                    if between:
                        between(k)

            def expert(u, U, E, **more):
                if not isinstance(E, int) or E >= 2:
                    pe.wait_ge(evac_done, E - 1)
                unit(main[u % 2], u % 2, U, **more)

            def logits(Q):
                def emit(k):
                    if k == 0:
                        pe.wait_ge(gw_rdy, Q + 1)
                        if not isinstance(Q, int) or Q:
                            pe.wait_ge(gt_evac, Q)
                    nc.tensor.matmul(gps[0][0:LOGIT_ROWS, :], gw[:, k, :], act_hi[:, k, :],
                                     start=(k == 0), stop=False, skip_group_check=True)
                    mm = nc.tensor.matmul(gps[0][0:LOGIT_ROWS, :], gw[:, k, :], act_lo[:, k, :],
                                          start=False, stop=(k == KT - 1), skip_group_check=True)
                    if k == KT - 1:
                        mm.then_inc(logit_done, 1)
                return emit

            def turn_logits(Q, R, shared):
                adder, n = (comb_sh, NE) if shared else (comb_tk, NG)

                def emit(k):
                    if k != 3:
                        return
                    pe.wait_ge(logit_evac, Q + 1)
                    pe.wait_ge(gw_in, shared if shared else gate_row(Q))
                    if not isinstance(R, int) or R:
                        pe.wait_ge(gb_rdy, R)
                    for bt in range(NBT):
                        mm = nc.tensor.matmul(gps[1][:, bt * n:(bt + 1) * n],
                                              logit_t[:, bt * P:(bt + 1) * P], adder, start=True, stop=True)
                    mm.then_inc(lt_done, 1)
                return emit

            def gate_row(Q):
                return gate_in_base[0] + Q * 32

            gate_in_base = [0]

            def turn_gates(Q):
                pe.wait_ge(g12_rdy, Q + 1)
                for bt in range(NBT):
                    mm = nc.tensor.matmul(gps[0][0:LOGIT_ROWS, bt * P:(bt + 1) * P], g12[:, bt, :], ident_r[:, :],
                                          start=True, stop=True)
                mm.then_inc(gt_done, 1)

            def broadcast(Q, R, order, places):
                def emit(k):
                    for n in [i for i, at in enumerate(places) if at == k]:
                        if n == 0:
                            pe.wait_ge(gt_evac, Q + 1)
                        if n >= 2:
                            pe.wait_ge(gb_rdy, R + n - 1)
                        j = order[n]
                        nc.tensor.matmul(gps[1 - n % 2][:, :], pick[:, j:j + 1].broadcast_to([12, P]),
                                         gate_t, start=True, stop=True).then_inc(bc_done, 1)
                return emit

            def gated_step(U, E, S, Q, R, order, shared=0):
                n = len(order)
                spread = [4, 4, 6, 7][:n] if n != 4 else [4, 4, 6, -1]
                expert(0, U, E, S=S, between=logits(Q))
                expert(1, U + 1, E + 1, between=turn_logits(Q, R, shared))
                bc = broadcast(Q, R, order, spread)

                def third(k):
                    if k == 1:
                        turn_gates(Q)
                    bc(k)

                expert(2, U + 2, E + 2, between=third)
                expert(3, U + 3, E + 3, between=broadcast(Q, R, order, [-1] * 4 + [1, 3] if n > 4 else [-1] * 3 + [1])
                       if n > 2 else None)
                with pe.Fori(0, 5) as i:
                    for c in range(2):
                        expert(c, U + 4 + c + i * 2, E + 4 + c + i * 2)
                expert(0, U + 14, E + 14)
                expert(1, U + 15, E + 15, last=True)

            def tower(U, S, stop=False):
                for m in range(MT1):
                    unit(top[m], m % 2, U + m, S=S if m == 0 else None, last=(m == MT1 - 1),
                         start=False, stop=stop)

            def tower2(h, U, S, banks):
                for d in range(2):
                    pe.wait_ge(hi_split, U + d + 1)
                    pe.wait_ge(lo_split, U + d + 1)
                    for c in range(2):
                        k = 2 * d + c
                        pe.wait_ge(act_hi_rdy, S * KT + 2 * (k + 1))
                        pe.wait_ge(act_lo_rdy, S * KT + 2 * (k + 1))
                        for m in range(MT2):
                            w = slice((c * MT2 + m) * P, (c * MT2 + m + 1) * P)
                            mm = three(banks[m][:, :], w_hi[:, d, w], w_lo[:, d, w], act_hi[:, k, :], act_lo[:, k, :],
                                       k == 0, k == MT1 - 1)
                            if k == MT1 - 1 and m == 0:
                                mm.then_inc(t2_done, 1)
                    mm.then_inc(unit_done, 1)
                for k in range(MT2):
                    pe.wait_ge(h2_rdy, h * MT2 + k + 1)
                    mm = nc.tensor.matmul(banks[2][0:1, :], w3[:, k:k + 1], eo_b[:, k, :],
                                          start=(k == 0), stop=(k == MT2 - 1))
                    if k == 0:
                        mm.then_inc(act_free, KT - 1)
                mm.then_inc(y_done, 1)

            pe.wait_ge(ident_rdy, 16)
            for bt in range(NBT):
                pe.wait_ge(x0_odd if bt % 2 else x0_even, bt // 2 + 1)
                for k in range(KT):
                    mm = nc.tensor.transpose(x0_bank[k][:, bt * P:(bt + 1) * P], ordered[bt][:, k * P:(k + 1) * P], ident)
                    if bt == NBT - 1:
                        mm.then_inc(x0_turned, 1)
            pe.wait_ge(pre_rdy, 1)
            pe.wait_ge(act_hi_rdy, 2)
            pe.wait_ge(act_lo_rdy, 2)
            for h in range(HALVES):
                (first, u0), (sf, s0), e0, q0, r0 = places(h), steps(h), h * EUNITS, h * GATED, h * BCASTS
                gate_in_base[0] = h * GATE_LOADS + 16 - q0 * 32
                gated_step(first, e0, sf, q0, r0, [4, 5], shared=h * GATE_LOADS + 16)
                if h:
                    tower2(h - 1, first + STEP, s0, top)
                with pe.Fori(0, T) as t:
                    gated_step(u0 + U_T0 + t * STEP, e0 + STEP + t * STEP, s0 + 1 + t, q0 + 1 + t, r0 + 2 + t * 6,
                               [4, 0, 2, 3, 5, 1])
                u, e = u0 + U_SH1, e0 + (T + 1) * STEP
                expert(0, u, e, S=s0 + T + 1)
                expert(1, u + 1, e + 1)
                with pe.Fori(0, 6) as i:
                    for c in range(2):
                        expert(c, u + 2 + c + i * 2, e + 2 + c + i * 2)
                expert(0, u + 14, e + 14)
                expert(1, u + 15, e + 15, last=True)
                if h:
                    pe.wait_ge(y_rdy, h)
                for d in range(2):
                    U = u0 + U_DENSE + d
                    pe.wait_ge(hi_split, U + 1)
                    pe.wait_ge(lo_split, U + 1)
                    for c in range(2):
                        w = slice(c * P, (c + 1) * P)
                        mm = three(top[2 * d + c][:, :], w_hi[0:DENSE, d, w], w_lo[0:DENSE, d, w],
                                   w_hi[0:DENSE, d, TOP1 // 2:DENSE_COLS], w_lo[0:DENSE, d, TOP1 // 2:DENSE_COLS], True, False)
                    mm.then_inc(unit_done, 1)
                own = [0, 2, 3, 1]
                e, s, q, r = e + STEP, s0 + T + 2, q0 + T + 1, r0 + 2 + 6 * T
                gated_step(u0 + U_T1, e, s, q, r, own)
                e, s, q, r, u = e + STEP, s + 1, q + 1, r + 4, u0 + U_T1N
                with pe.Fori(0, T - 2) as t:
                    gated_step(u + t * (STEP + MT1), e + t * STEP, s + t * 2, q + t, r + t * 4, own)
                    tower(u + STEP + t * (STEP + MT1), s + 1 + t * 2)
                n = T - 2
                u, e, s, q, r = u + n * (STEP + MT1), e + n * STEP, s + 2 * n, q + n, r + 4 * n
                gated_step(u, e, s, q, r, own)
                tower(u + STEP, s + 1)
                tower(u + STEP + MT1, s + 2, stop=True)
            pe.wait_ge(evac_done, HALVES * EUNITS)
            tower2(HALVES - 1, u + STEP + 2 * MT1, s + 3, main + gps)

        @block.scalar
        def _(act):
            def split_hi(slot, rawslot, turn, parts=P, cols=KT * P):
                act.wait_ge(raw_in[rawslot], turn * 16 + 16)
                nc.scalar.activation(w_hi[0:parts, slot, 0:cols], raw[0:parts, rawslot, 0:cols], ACT.Copy)\
                    .then_inc(hi_split, 1)

            def evacuate(src, dst, bias):
                nc.scalar.activation(dst, src, ACT.Relu, bias=bias).then_inc(evac_done, 1)

            def hand_over(S, chunk, ks, U):
                for k in ks:
                    if not isinstance(S, int) or S:
                        if k < KT - 1:
                            act.wait_ge(act_free, (S - 1) * (KT - 1) + k + 1)
                        else:
                            act.wait_ge(unit_done, U)
                    nc.scalar.activation(act_hi[:, bass.ds(k, 1), :], slots[:, bass.ds(chunk + k, 1), :],
                                         ACT.Copy).then_inc(act_hi_rdy, 1)

            def gate_copies(R, first, last, order, Pb):
                for n in range(first, last):
                    act.wait_ge(bc_done, R + n + 1)
                    if n == first > 0:
                        act.wait_ge(pair_done, Pb)
                    nc.scalar.activation(gate_b[:, order[n], :], gps[1 - n % 2][:, :], ACT.Copy).then_inc(gb_rdy, 1)

            def gate_slot(j, Q, R, rows_, order, Pb):
                if j == 0:
                    act.wait_ge(logit_done, Q + 1)
                    if not isinstance(Q, int) or Q:
                        act.wait_ge(lt_done, Q)
                    nc.scalar.activation(logit_t[0:rows_, :], gps[0][0:rows_, :], ACT.Copy).then_inc(logit_evac, 1)
                n = min(4, len(order)) - (len(order) == 4)
                if j == 1:
                    act.wait_ge(shift_rdy, Q + 1)
                    nc.scalar.activation(lg[:, :, 0:rows_ // 2], lg[:, :, 0:rows_ // 2], ACT.Exp).then_inc(exp_rdy, 1)
                if j == 2:
                    act.wait_ge(gt_done, Q + 1)
                    if not isinstance(R, int) or R:
                        act.wait_ge(bc_done, R)
                    nc.scalar.activation(gate_t, gps[0][0:12, :], ACT.Copy).then_inc(gt_evac, 1)
                    if not isinstance(Pb, int) or Pb > 8:
                        act.wait_ge(pair_done, Pb - 4)
                    gate_copies(R, 0, n, order, Pb)
                if j == 3:
                    gate_copies(R, n, len(order), order, Pb)

            def step(U, V, off, dest, bias, gates=None):
                for j in range(1, STEP - 1):
                    if j == 1 and gates:
                        gate_slot(0, *gates)
                    act.wait_ge(unit_done, U + j)
                    split_hi((j + 1) % 2, (off + j + 1) % RAW, V + (off + j + 1) // RAW)
                    dest_wait(dest, j - 1)
                    evacuate(main[(j - 1) % 2][:, :], dest(j - 1), bias(j - 1))
                    if gates:
                        gate_slot(j, *gates)

            def dest_wait(dest, u):
                if u in dest.waits:
                    for s_, v in dest.waits[u]:
                        act.wait_ge(s_, v)

            def shared_dest(waits):
                def dest(u):
                    return eo_sh[:, u, :]
                dest.waits = waits
                return dest

            def task_dest(t, S, Pb):
                def dest(u):
                    if u < KT:
                        return slots[:, bass.ds(t * KT + u, 1), :]
                    return eo_b[:, bass.ds(u % 4, 1), :]
                dest.waits = {
                    0: [(act_lo_rdy, (S + 1) * KT)],
                    KT: [(pair_done, Pb)],
                    KT + 4: [(pair_done, Pb + 5)],
                    KT + 6: [(pair_done, Pb + 6)],
                }
                return dest

            def biases(tile, first):
                return lambda u: tile[:, bass.ds(first + u, 1)]

            def change(U, V, off, dest, bias, S, chunk, shared=None):
                act.wait_ge(unit_done, U - 1)
                split_hi(0, off % RAW, V)
                dest_wait(dest, STEP - 2)
                evacuate(main[0][:, :], dest(STEP - 2), bias(STEP - 2))
                if shared:
                    for p in range(3):
                        act.wait_ge(sh_done, shared + p)
                        hand_over(S, chunk, (2 * p, 2 * p + 1), U)
                else:
                    hand_over(S, chunk, range(KT), U)
                act.wait_ge(unit_done, U)
                dest_wait(dest, STEP - 1)
                evacuate(main[1][:, :], dest(STEP - 1), bias(STEP - 1))
                split_hi(1, (off + 1) % RAW, V + (off + 1) // RAW)
                if shared:
                    act.wait_ge(sh_done, shared + 3)
                    hand_over(S, chunk, (6, 7), U)

            def first_step_out(h, U, dest, bias, S):
                V, off = U // RAW, U % RAW
                act.wait_ge(unit_done, U - 1)
                split_hi(0, off, V)
                evacuate(main[0][:, :], dest(STEP - 2), bias(STEP - 2))
                act.wait_ge(x_done, set_no(h, ROWSETS))
                if h == 0:
                    hand_over(S, 0, range(KT), U)
                else:
                    first_outputs(h - 1, S - 1, top)
                act.wait_ge(unit_done, U)
                split_hi(1, off + 1, V)
                evacuate(main[1][:, :], dest(STEP - 1), bias(STEP - 1))
                if h == 0:
                    return
                V, off = (U + 2) // RAW, (U + 2) % RAW
                act.wait_ge(unit_done, U + 1)
                split_hi(0, off, V)
                second_outputs(h - 1, U, top)
                split_hi(1, off + 1, V)
                for k in range(KT):
                    nc.scalar.activation(act_hi[:, k, :], slots[:, k, :], ACT.Copy).then_inc(act_hi_rdy, 1)
                result(h - 1, top)

            def first_sums(h):
                act.wait_ge(pair_done, (h + 1) * PAIRS)
                for m in range(MT1):
                    act.wait_ge(unit_done, places(h + 1)[0] + (2 if h else 0) - MT1 + m + 1)
                    nc.scalar.activation(gate_b[:, m, :], top[m][:, :], ACT.Relu, bias=bias_t1[:, m:m + 1])\
                        .then_inc(h1_rdy, 1)

            def first_outputs(h, S, banks):
                for k in range(MT1):
                    act.wait_ge(h1_rdy, h * MT1 + k + 1)
                    act.wait_ge(act_free, (S - 1) * (KT - 1) + k + 1)
                    nc.scalar.activation(act_hi[:, k, :], gate_b[:, k, :], ACT.Copy).then_inc(act_hi_rdy, 2)

            def second_outputs(h, U, banks):
                for m in range(MT2):
                    if m == 0:
                        act.wait_ge(t2_done, h + 1)
                    else:
                        act.wait_ge(unit_done, U + 2)
                    nc.scalar.activation(eo_b[:, m, :], banks[m][:, :], ACT.Relu, bias=bias_t2[:, m:m + 1])\
                        .then_inc(h2_rdy, 1)

            def result(h, banks):
                act.wait_ge(y_done, h + 1)
                act.wait_ge(lt_done, (h + 1) * GATED + (h + 1 < HALVES))
                nc.scalar.activation(logit_t[0:1, :], banks[2][0:1, :], ACT.Copy).then_inc(y_rdy, 1)
                act.wait_ge(y_rdy, h + 1)
                act.dma_start(out[h:h + 1, :], logit_t[0:1, :]).then_inc(y_out, 16)
                act.wait_ge(y_out, 16 * (h + 1))

            def tower_slots(U, V, off, S, chunk, needs=None, last=False):
                for j in (1, 2):
                    act.wait_ge(unit_done, U + j)
                    split_hi((j + 1) % 2, (off + j + 1) % RAW, V + (off + j + 1) // RAW)
                act.wait_ge(unit_done, U + 3)
                split_hi(0, off, V + 1)
                if last:
                    return
                if needs:
                    act.wait_ge(*needs)
                hand_over(S, chunk, range(KT), U + 4)
                act.wait_ge(unit_done, U + 4)
                split_hi(1, (off + 1) % RAW, V + 1 + (off + 1) // RAW)

            for dst, src in ((bias0, b0), (bias1, b1), (bias_t1, b_top1), (bias_t2, b_top2), (w3, w_top3)):
                act.dma_start(dst[:, :], src).then_inc(consts_in, 16)
            act.dma_start(comb_sh[0:ONES_ROW, :], comb_s).then_inc(consts_in, 16)
            act.dma_start(comb_sh[ONES_ROW:ONES_ROW + 1, :], gs_b).then_inc(consts_in, 16)
            act.dma_start(comb_tk[0:ONES_ROW, :], comb_t).then_inc(consts_in, 16)
            act.wait_ge(chain, 4)
            nc.scalar.activation(warm[:, 1:2], warm[:, 0:1], ACT.Exp)
            split_hi(0, 0, 0)
            for i in (1, 3):
                act.wait_ge(x0_in[i], 16)
                nc.scalar.activation(*by_order(i), ACT.Copy).then_inc(x0_odd, 1)
            split_hi(1, 1, 0)
            for k in range(KT):
                act.wait_ge(x0_turned, k + 1)
                nc.scalar.activation(act_hi[:, k, :], x0_bank[k][:, :], ACT.Copy).then_inc(act_hi_rdy, 1)
            act.wait_ge(pre_rdy, 1)
            act.wait_ge(consts_in, 16 * 8)
            for h in range(HALVES):
                (first, u0), (sf, s0), q0, r0, p0 = places(h), steps(h), h * GATED, h * BCASTS, h * PAIRS
                v0 = u0 // RAW
                dest, bias = shared_dest({0: [(pair_done, p0)]} if h else {}), biases(bias0, 0)
                step(first, first // RAW, first % RAW, dest, bias, (q0, r0, 2 * NE, [4, 5], p0))
                first_step_out(h, first + STEP, dest, bias, s0 + 1)

                def task0(t, shared=None):
                    U, V = u0 + U_T0 + t * STEP, (u0 + U_T0) // RAW + t * (STEP // RAW)
                    S, Pb = s0 + 1 + t, p0 + 8 + t * 8
                    dest, bias = task_dest(t, S, Pb), biases(bias0, STEP + t * STEP)
                    step(U, V, 0, dest, bias, (q0 + 1 + t, r0 + 2 + t * 6, 2 * NG, [4, 0, 2, 3, 5, 1], Pb))
                    change(U + STEP, V + STEP // RAW, 0, dest, bias, S + 1, (t + 1) * KT, shared=shared)

                with act.Fori(0, T - 1) as t:
                    task0(t)
                task0(T - 1, shared=h * 4 * T + 1 + (T - 1) * 4)
                U, S = u0 + U_SH1, s0 + T + 1
                V = U // RAW
                dest, bias = shared_dest({0: [(pair_done, p0 + 8 * T + 4)]}), biases(bias1, 0)
                step(U, V, 0, dest, bias)
                D0 = u0 + U_DENSE
                act.wait_ge(unit_done, D0 - 1)
                act.wait_ge(dctx_in[0], 16 * (h + 1))
                split_hi(0, 0, D0 // RAW, parts=DENSE, cols=DENSE_COLS)
                evacuate(main[0][:, :], dest(STEP - 2), bias(STEP - 2))
                hand_over(S + 1, 0, range(KT), D0)
                act.wait_ge(unit_done, D0)
                act.wait_ge(dctx_in[1], 16 * (h + 1))
                split_hi(1, 1, D0 // RAW, parts=DENSE, cols=DENSE_COLS)
                U, V, off = u0 + U_T1, (u0 + U_T1) // RAW, U_T1 % RAW
                act.wait_ge(unit_done, U - 1)
                split_hi(0, off, V)
                evacuate(main[1][:, :], dest(STEP - 1), bias(STEP - 1))
                act.wait_ge(unit_done, U)
                split_hi(1, off + 1, V)
                own = [0, 2, 3, 1]
                S, Pb, Q, R = S + 1, p0 + 8 * (T + 1), q0 + T + 1, r0 + 2 + 6 * T
                dest, bias = task_dest(0, S, Pb), biases(bias1, STEP)
                step(U, V, off, dest, bias, (Q, R, 2 * NG, own, Pb))
                change(U + STEP, V + STEP // RAW, off, dest, bias, S + 1, KT)
                Un, Vn = u0 + U_T1N, V + STEP // RAW
                both = STEP + MT1

                def task1(n, last=False):
                    t, Sn, Pn, Ut, Vt = n + 1, S + 1 + n * 2, Pb + 8 + n * 8, Un + n * both, Vn + n * (both // RAW)
                    dest, bias = task_dest(t, Sn, Pn), biases(bias1, STEP + t * STEP)
                    step(Ut, Vt, off, dest, bias, (Q + 1 + n, R + 4 + n * 4, 2 * NG, own, Pn))
                    change(Ut + STEP, Vt + STEP // RAW, off, dest, bias, Sn + 1, (t - 1) * KT)
                    tower_slots(Ut + STEP, Vt + STEP // RAW, off, Sn + 2, (t if last else t + 1) * KT,
                                needs=(pair_done, Pn + 8) if last else None)

                with act.Fori(0, T - 2) as n:
                    task1(n)
                task1(T - 2, last=True)
                U = Un + (T - 1) * both
                if h + 1 < HALVES:
                    tower_slots(U, U // RAW, off, steps(h + 1)[0], 4 * KT,
                                needs=(x_done, set_no(h + 1, NBT)))
                    first_sums(h)
            tower_slots(U, U // RAW, off, None, None, last=True)
            first_sums(HALVES - 1)
            S, U = s0 + HALF_STEPS, U + MT1
            first_outputs(HALVES - 1, S, main + gps)
            act.wait_ge(unit_done, U)
            split_hi(1, (off + 1) % RAW, U // RAW + (off + 1) // RAW)
            second_outputs(HALVES - 1, U, main + gps)
            result(HALVES - 1, main + gps)

        @block.vector
        def _(dve):
            class Count:
                start, n = 0, 0

            links = Count()

            def link(ins):
                links.n += 1
                ins.then_inc(chain, 1)
                return links.start + links.n

            def after(value):
                dve.wait_ge(chain, value)

            def split_lo(U, slot, rawslot, turn, parts=P, cols=KT * P):
                dve.wait_ge(raw_in[rawslot], turn * 16 + 16)
                dve.wait_ge(hi_split, U + 1)
                nc.vector.tensor_tensor(w_lo[0:parts, slot, 0:cols], raw[0:parts, rawslot, 0:cols],
                                        w_hi[0:parts, slot, 0:cols], ALU.subtract).then_inc(lo_split, 1)

            def hand_over(S, chunk, ks):
                for k in ks:
                    dve.wait_ge(act_hi_rdy, S * KT + k + 1)
                    nc.vector.tensor_tensor(act_lo[:, bass.ds(k, 1), :], slots[:, bass.ds(chunk + k, 1), :],
                                            act_hi[:, bass.ds(k, 1), :], ALU.subtract).then_inc(act_lo_rdy, 1)

            def split_gates(q_in, Q, n, R):
                dve.wait_ge(gw_in, q_in)
                if not isinstance(Q, int) or Q:
                    dve.wait_ge(logit_done, Q)
                    dve.wait_ge(gb_rdy, R)
                src = gw_raw[:, 0:KT * n].rearrange("p (k n) -> p k n", k=KT)
                nc.vector.tensor_copy(gw[:, :, 0:n], src).then_inc(gw_step, 1)
                dve.wait_ge(gw_step, Q + 1)
                nc.vector.tensor_tensor(gw[:, :, n:2 * n], src, gw[:, :, 0:n], ALU.subtract).then_inc(gw_rdy, 1)

            def softmax(Q, n, shared_at=None):
                t = slice(0, n)
                dve.wait_ge(lt_done, Q + 1)
                ps = gps[1][:, 0:NBT * n].rearrange("p (b n) -> p b n", b=NBT)
                after(link(nc.vector.tensor_reduce(mx[:, :], ps, AX.X, ALU.max)))
                nc.vector.tensor_tensor(lg[:, :, t], ps, mx[:, :, None].broadcast_to([P, NBT, n]),
                                        ALU.subtract).then_inc(shift_rdy, 1)
                dve.wait_ge(exp_rdy, Q + 1)
                after(link(nc.vector.tensor_reduce(mx[:, :], lg[:, :, t], AX.X, ALU.add)))
                after(link(nc.vector.reciprocal(rs[:, :], mx[:, :])))
                inv = rs[:, :, None].broadcast_to([P, NBT, n])
                if n == NE:
                    after(link(nc.vector.tensor_tensor(gsh[:, :, :], lg[:, :, t], inv, ALU.mult)))
                    last = link(nc.vector.tensor_copy(g6[:, :, 4:6], gsh[:, :, NE - 2:NE]))
                else:
                    last = link(nc.vector.tensor_tensor(g6[:, :, 0:n], lg[:, :, t], inv, ALU.mult))
                    if shared_at is not None:
                        last = link(nc.vector.tensor_copy(g6[:, :, 4:6], gsh[:, :, bass.ds(shared_at, 2)]))
                after(last)
                after(link(nc.vector.tensor_copy(g12[:, :, 0:6], g6[:, :, :])))
                nc.vector.tensor_tensor(g12[:, :, 6:12], g6[:, :, :], g12[:, :, 0:6], ALU.subtract)\
                    .then_inc(g12_rdy, 1)

            def gate(j):
                return gate_b[:, j:j + 1, :].broadcast_to([P, 2, N])

            def gating(kind, t, E, R, Pb, shb=None):
                tmp = prod[:, :, :]
                order = {"shared": [4, 5], "layer0": [4, 0, 2, 3, 5, 1], "layer1": [0, 2, 3, 1]}[kind]
                seen = {}

                def pair(first, p):
                    return slots[:, bass.ds(first * KT + 2 * p, 2), :]

                def sh(x, p):
                    return eo_sh[:, x * KT + 2 * p:x * KT + 2 * p + 2, :]

                def out_of_psum(u):
                    dve.wait_ge(evac_done, E + u + 2)

                def mul(dst, src, j, name, needs):
                    dve.wait_ge(gb_rdy, R + order.index(j) + 1)
                    for n in needs:
                        wait(n)
                    seen[name] = (chain, link(nc.vector.tensor_tensor(dst, src, gate(j), ALU.mult)))

                def add(dst, x, needs, name, signal=None):
                    for n in needs:
                        wait(n)
                    ins = nc.vector.tensor_tensor(dst, dst, x, ALU.add)
                    if signal is None:
                        signal = (chain, link(ins))
                    else:
                        ins.then_inc(signal[0], 1)
                    seen[name] = signal

                def wait(name):
                    if name in seen:
                        dve.wait_ge(*seen[name])

                if not isinstance(Pb, int) or Pb:
                    seen["tmp read"] = (pair_done, Pb)

                def a_ops(p):
                    done = (pair_done, Pb + p + 1)
                    if kind == "shared":
                        def first():
                            out_of_psum(2 * p)
                            dve.wait_ge(gb_rdy, R + 1)
                            nc.vector.tensor_tensor(pair(4, p), sh(0, p), gate(4), ALU.mult).then_inc(pair_done, 1)
                        return [first]
                    a = pair(t, p)
                    if kind == "layer1":
                        return [
                            lambda: (out_of_psum(2 * p), mul(a, a, 0, "own", [])),
                            lambda: mul(tmp, sh(0, p), 2, "s8", ["tmp read"]),
                            lambda: add(a, tmp, ["s8"], "tmp read"),
                            lambda: mul(tmp, sh(1, p), 3, "s9", ["tmp read"]),
                            lambda: add(a, tmp, ["s9"], "tmp read", done),
                        ]
                    return [
                        lambda: (out_of_psum(2 * p), mul(tmp, a, 4, "sh", ["tmp read"])),
                        lambda: add(pair(4, p), tmp, ["sh"], "tmp read"),
                        lambda: mul(a, a, 0, "own", ["sh"]),
                        lambda: mul(tmp, sh(0, p), 2, "s8", ["tmp read"]),
                        lambda: add(a, tmp, ["s8"], "tmp read"),
                        lambda: mul(tmp, sh(1, p), 3, "s9", ["tmp read"]),
                        lambda: add(a, tmp, ["s9"], "tmp read", done),
                    ]

                def b_ops(p):
                    done = (pair_done, Pb + 5 + p)

                    def gated_first(then):
                        dve.wait_ge(pair_done, Pb + p + 1)
                        then()

                    if kind == "shared":
                        return [lambda: (out_of_psum(KT + 2 * p), mul(tmp, sh(1, p), 5, "sh", ["tmp read"])),
                                lambda: gated_first(lambda: add(pair(4, p), tmp, ["sh"], "tmp read", done))]
                    b = eo_b[:, 2 * (p % 2):2 * (p % 2) + 2, :]
                    own = lambda: gated_first(lambda: add(pair(t, p), b, ["own"], "own done", done))
                    if kind == "layer1":
                        return [lambda: (out_of_psum(KT + 2 * p), mul(b, b, 1, "own", [])), own]
                    return [lambda: (out_of_psum(KT + 2 * p), mul(tmp, b, 5, "sh", ["tmp read"])),
                            lambda: add(pair(4, p), tmp, ["sh"], "tmp read", (sh_done, shb + p + 1)),
                            lambda: mul(b, b, 1, "own", ["sh"]), own]

                return a_ops, b_ops

            def transpose_rows(h, g):
                t, bt = rows(g)
                dve.wait_ge(x_in[g % 2], 16 * Q4 * (set_no(h, g) // 2 + 1))
                for s in range(Q4):
                    at = bt * P + s * 32
                    ins = nc.vector.transpose(slots[:, t * KT:(t + 1) * KT, at:at + 32], stage(g)[:, s, :])
                ins.then_inc(x_done, 1)

            def run(ops):
                for op in ops:
                    op()

            def step(U, V, off, ops=None, gates=None, split=None, plan=None, late=(), x=None):
                sets = iter(range(NBT, ROWSETS))
                queue = []
                if plan:
                    for p in range(4):
                        queue += ops[0](p)
                    for p in range(3):
                        queue += ops[1](p)
                for j in range(1, STEP - 1):
                    split_lo(U + j + 1, (j + 1) % 2, (off + j + 1) % RAW, V + (off + j + 1) // RAW)
                    if j == 1 and gates:
                        softmax(*gates)
                    if j == 2:
                        run(late)
                    if j == 8 and split:
                        split_gates(*split)
                    if x is not None:
                        for _ in range(2 if j in (10, 14) else 1):
                            transpose_rows(x, next(sets))
                    if plan and j >= 3:
                        done = sum(plan[:j - 3])
                        run(queue[done:done + plan[j - 3]])
                    elif ops and j >= 3:
                        p, second = (j - 3) // 2, (j - 3) % 2
                        now = ops[0](p) if p < 4 else ops[1](p - 4)
                        cut = (len(now) + 1) // 2
                        run(now[cut:] if second else now[:cut])

            def change(U, V, off, S, chunk, ops, shared=False):
                split_lo(U, 0, off, V)
                b2, b3 = ops[1](2), ops[1](3)
                if shared:
                    hand_over(S, chunk, range(0, 6))
                    run(b3[:2])
                    hand_over(S, chunk, (6, 7))
                    split_lo(U + 1, 1, off + 1, V)
                    return b2[2:] + b3[2:]
                hand_over(S, chunk, range(KT))
                split_lo(U + 1, 1, off + 1, V)
                run(b2 + b3)

            def tower_slots(U, V, off, S, chunk, last=False, x=None):
                for j in (1, 2):
                    split_lo(U + j + 1, (j + 1) % 2, (off + j + 1) % RAW, V + (off + j + 1) // RAW)
                    if x is not None:
                        transpose_rows(x, 2 * j - 2)
                        transpose_rows(x, 2 * j - 1)
                split_lo(U + 4, 0, off, V + 1)
                if not last:
                    hand_over(S, chunk, range(KT))
                    split_lo(U + 5, 1, (off + 1) % RAW, V + 1 + (off + 1) // RAW)

            def first_outputs(S):
                for k in range(MT1):
                    dve.wait_ge(act_hi_rdy, S * KT + 2 * (k + 1))
                    nc.vector.tensor_tensor(act_lo[:, k, :], gate_b[:, k, :], act_hi[:, k, :], ALU.subtract)\
                        .then_inc(act_lo_rdy, 2)

            def loop_links(i, per):
                begun = links.start + links.n
                links.start, links.n = begun + i * per, 0
                return begun

            def end_links(begun, turns, per):
                assert links.n == per, (links.n, per)
                links.start, links.n = begun + turns * per, 0

            nc.vector.memset(gw[:, :, :].bitcast(f32), 0.0).then_inc(chain, 1)
            nc.vector.memset(logit_t[:, :], 1.0).then_inc(chain, 1)
            nc.vector.memset(g6[:, :, :], 0.0).then_inc(chain, 1)
            nc.vector.memset(warm[:, :], 0.0).then_inc(chain, 1)
            nc.vector.memset(g12[:, :, :].bitcast(f32), 0.0).then_inc(chain, 1)
            links.n = 5
            after(5)
            dve.wait_ge(idx_in, 16)
            for q in range(Q4):
                part = idx[q * 32:(q + 1) * 32, NBT:]
                nc.vector.tensor_scalar(part, part, float(Q4), float(q), ALU.mult, ALU.add).then_inc(idx_rdy, 1)

            def put_in_order(i):
                dve.wait_ge(x0_in[i], 16)
                nc.vector.tensor_copy(*by_order(i)).then_inc(x0_even, 1)

            put_in_order(0)
            dve.wait_ge(ident_rdy, 16)
            after(link(nc.vector.tensor_tensor(pick[:, :], prod[0:12, 0, 0:6], prod[0:12, 0, 6:12], ALU.add)))
            nc.vector.tensor_copy(ident_r[:, :], ident).then_inc(pre_rdy, 1)
            dve.wait_ge(pre_rdy, 1)
            put_in_order(2)
            split_gates(16, 0, NE, 0)
            split_lo(0, 0, 0, 0)
            split_lo(1, 1, 1, 0)
            for k in range(KT):
                dve.wait_ge(act_hi_rdy, k + 1)
                nc.vector.tensor_tensor(act_lo[:, k, :], x0_bank[k][:, :], act_hi[:, k, :], ALU.subtract)\
                    .then_inc(act_lo_rdy, 1)
            plan0 = [3, 3, 3, 3, 4, 3, 3, 3, 4, 3, 2, 2]
            plan0_last = plan0[:10] + [3, 3]
            for h in range(HALVES):
                (first, u0), (sf, s0), e0, q0, r0, p0 = \
                    places(h), steps(h), h * EUNITS, h * GATED, h * BCASTS, h * PAIRS
                gin = h * GATE_LOADS + 16
                ops = gating("shared", 4, e0, r0, p0)
                step(first, first // RAW, first % RAW, ops, (q0, NE), (gin + 32, q0 + 1, NG, r0 + 2), x=h)
                U = first + STEP
                if h == 0:
                    change(U, U // RAW, U % RAW, s0 + 1, 0, ops)
                else:
                    split_lo(U, 0, U % RAW, U // RAW)
                    first_outputs(s0)
                    split_lo(U + 1, 1, (U + 1) % RAW, U // RAW)
                    run(ops[1](2))
                    change(U + 2, (U + 2) // RAW, 0, s0 + 1, 0, (None, lambda p: ops[1](3) if p == 3 else []))

                def task0(t, plan, last=False):
                    U, V = u0 + U_T0 + t * STEP, (u0 + U_T0) // RAW + t * (STEP // RAW)
                    ops = gating("layer0", t, e0 + STEP + t * STEP, r0 + 2 + t * 6, p0 + 8 + t * 8,
                                 h * 4 * T + t * 4)
                    step(U, V, 0, ops, (q0 + 1 + t, NG, t * 2), (gin + 64 + t * 32, q0 + 2 + t, NG, r0 + 8 + t * 6),
                         plan)
                    return change(U + STEP, V + STEP // RAW, 0, s0 + 2 + t, (t + 1) * KT, ops, shared=last)

                with dve.Fori(0, T - 1) as t:
                    begun = loop_links(t, LINKS_L0)
                    task0(t, plan0)
                end_links(begun, T - 1, LINKS_L0)
                left = task0(T - 1, plan0_last, last=True)
                U = u0 + U_SH1
                step(U, U // RAW, 0, late=left)
                D0, U, off = u0 + U_DENSE, u0 + U_T1, U_T1 % RAW
                V, S = U // RAW, s0 + T + 2
                dve.wait_ge(dctx_in[0], 16 * (h + 1))
                split_lo(D0, 0, 0, D0 // RAW, parts=DENSE, cols=DENSE_COLS)
                hand_over(S, 0, range(KT))
                dve.wait_ge(dctx_in[1], 16 * (h + 1))
                split_lo(D0 + 1, 1, 1, D0 // RAW, parts=DENSE, cols=DENSE_COLS)
                split_lo(U, 0, off, V)
                split_lo(U + 1, 1, off + 1, V)
                E, R, Pb, Q = e0 + (T + 2) * STEP, r0 + 2 + 6 * T, p0 + 8 * (T + 1), q0 + T + 1
                gin = gin + 32 * (T + 2)
                ops = gating("layer1", 0, E, R, Pb)
                step(U, V, off, ops, (Q, NG), (gin, Q + 1, NG, R + 4))
                change(U + STEP, V + STEP // RAW, off, S + 1, KT, ops)
                Un, Vn, both = U + STEP, V + STEP // RAW, STEP + MT1

                def task1(n, split, last=False):
                    t, Sn, Ut, Vt = n + 1, S + 1 + n * 2, Un + n * both, Vn + n * (both // RAW)
                    ops = gating("layer1", t, E + STEP + n * STEP, R + 4 + n * 4, Pb + 8 + n * 8)
                    step(Ut, Vt, off, ops, (Q + 1 + n, NG), split)
                    change(Ut + STEP, Vt + STEP // RAW, off, Sn + 1, (t - 1) * KT, ops)
                    tower_slots(Ut + STEP, Vt + STEP // RAW, off, Sn + 2, (t if last else t + 1) * KT)

                with dve.Fori(0, T - 2) as n:
                    begun = loop_links(n, LINKS_L1)
                    task1(n, (gin + 32 + n * 32, Q + 2 + n, NG, R + 8 + n * 4))
                end_links(begun, T - 2, LINKS_L1)
                more = h + 1 < HALVES
                task1(T - 2, ((h + 1) * GATE_LOADS + 16, (h + 1) * GATED, NE, (h + 1) * BCASTS) if more else None,
                      last=True)
                U = Un + (T - 1) * both
                if more:
                    tower_slots(U, U // RAW, off, steps(h + 1)[0], 4 * KT, x=h + 1)
            tower_slots(U, U // RAW, off, None, None, last=True)
            first_outputs(s0 + HALF_STEPS)
            U += MT1
            split_lo(U + 1, 1, (off + 1) % RAW, (U + 1) // RAW)


LINKS_L0 = 6 + 4 * 6 + 4 * 2
LINKS_L1 = 5 + 4 * 4 + 4 * 1


def _quarters(w):
    e, _, n = w.shape
    return w.reshape(e, Q4, KT, 32, n).transpose(0, 2, 1, 3, 4).reshape(e, D, n)


def _units(w, strips):
    e, k, _ = w.shape
    return np.ascontiguousarray(
        w.reshape(e, k // P, P, strips, P).transpose(0, 3, 2, 1, 4).reshape(e * strips, P, k))


def kernel(dense_ctx, ids, tbl_0, tbl_1, tbl_2, tbl_3, tbl_4, W_top1, b_top1, W_top2, b_top2, W_top3,
           L0_rec_W0, L0_rec_b0, L0_rec_G0w, L0_rec_G0b, L0_rec_Gs0w, L0_rec_Gs0b, L0_rec_W1, L0_rec_b1,
           L0_rec_G1w, L0_rec_G1b):
    import concourse.bacc as bacc
    from concourse.bass_utils import run_bass_kernel_spmd as run

    a = {k: np.asarray(v) for k, v in locals().items() if k not in ("bacc", "run")}
    order = list(EXPERTS)

    def kt_cols(w):
        k, n = w.shape
        return np.ascontiguousarray(w.reshape(k // P, P, n).transpose(1, 0, 2).reshape(P, -1))

    def per_part(v):
        return np.ascontiguousarray(v.reshape(-1, P).T)

    def combine(n):
        c = np.zeros((ONES_ROW, n), np.float32)
        c[np.arange(2 * n), np.arange(2 * n) % n] = 1.0
        return c

    by_table = a["ids"].T
    quarter_ids = np.concatenate([by_table[:T].reshape(-1, 32), by_table[T, N:].reshape(-1, 32)]).T
    w_top1 = a["W_top1"]
    laid = {
        "ids": np.concatenate([by_table[T, :N].reshape(NBT, P).T, np.tile(quarter_ids, (Q4, 1))], axis=1),
        "dense_t": np.ascontiguousarray(a["dense_ctx"].T),
        "tbl_0": a["tbl_0"], "tbl_1": a["tbl_1"], "tbl_2": a["tbl_2"], "tbl_3": a["tbl_3"], "tbl_4": a["tbl_4"],
        "w0": _units(_quarters(a["L0_rec_W0"][order]), KT),
        "w1": _units(a["L0_rec_W1"][order], KT),
        "w_top": _units(w_top1[:T * D].reshape(T, D, TOP1), MT1),
        "w_dense": np.ascontiguousarray(w_top1[T * D:].reshape(DENSE, 2, TOP1 // 2).transpose(1, 0, 2)),
        "w_top2": np.ascontiguousarray(
            a["W_top2"].reshape(2, 2, P, TOP2).transpose(0, 2, 1, 3).reshape(2, P, 2 * TOP2)),
        "w_top3": per_part(a["W_top3"]),
        "b0": per_part(a["L0_rec_b0"][order]), "b1": per_part(a["L0_rec_b1"][order]),
        "b_top1": per_part(a["b_top1"]), "b_top2": per_part(a["b_top2"]),
        "gs_w": kt_cols(_quarters(a["L0_rec_Gs0w"][None])[0]),
        "g_w": np.stack([kt_cols(w) for w in (*_quarters(a["L0_rec_G0w"]), *a["L0_rec_G1w"])]),
        "g_b": np.concatenate([a["L0_rec_G0b"], a["L0_rec_G1b"]]),
        "comb_s": combine(NE), "comb_t": combine(NG),
        "gs_b": a["L0_rec_Gs0b"].reshape(1, NE),
        "ident_in": np.eye(P, dtype=np.float32),
    }
    nc = bacc.Bacc("TRN2", target_bir_lowering=False, num_devices=1)
    args = {n: nc.dram_tensor(f"in_{n}", v.shape, mybir.dt.from_np(v.dtype), kind="ExternalInput").ap()
            for n, v in laid.items()}
    y = nc.dram_tensor("y", (HALVES, N), mybir.dt.float32, kind="ExternalOutput").ap()
    build(nc, out=y, **args)
    r = run(nc, [{f"in_{n}": v for n, v in laid.items()}], core_ids=[0])
    return np.asarray(r.results[0]["y"]).reshape(B, 1)
```
